# Optimizing a Trainium2 kernel written in Bass

```python
import numpy as np
import jax
import jax.numpy as jnp

def _softmax(x, axis=-1):
    return jax.nn.softmax(x, axis=axis)

def _gelu(x):
    return jax.nn.gelu(x, approximate=True)

def _silu(x):
    return jax.nn.silu(x)

def _sigmoid(x):
    return jax.nn.sigmoid(x)

def _layernorm(x, axis=-1, eps=1e-05):
    m = jnp.mean(x, axis=axis, keepdims=True)
    v = jnp.var(x, axis=axis, keepdims=True)
    return (x - m) / jnp.sqrt(v + eps)

def _scatter_add(tgt, idx, src, axis=0):
    return tgt.at[idx].add(src)

def _segment_sum(src, seg, n):
    return jax.ops.segment_sum(src, seg, n)
kernel_name = 'mk_conv_preact_d2_conv_nchw32_r2_93db34'

def setup_inputs(seed: int=0):
    np.random.seed(seed)
    _w = jnp.asarray

    def _rec_inputs():
        import jax
        import jax.numpy as jnp
        _gk = jax.random.key(seed)
        x = -7.109e-05 + 0.9999 * jax.random.normal(jax.random.fold_in(_gk, 1), (8, 32, 256, 256), jnp.float32)
        return x
    x = _rec_inputs()

    def _L0_conv_setup():
        import jax, jax.numpy as jnp
        import numpy as np
        R = 5
        ALPHA = 0.65
        NEG = -1e+30

        def _harmonic_basis(theta, K):
            feats = []
            for k in range(1, K + 1):
                m = (k + 1) // 2
                feats.append(jnp.cos(m * theta) if k % 2 == 1 else jnp.sin(m * theta))
            return jnp.stack(feats, axis=-1)

        def morphological_kernel(finsler_params, r, alpha):
            coords = jnp.arange(-r, r + 1, dtype=jnp.float32)
            yy, xx = jnp.meshgrid(coords, coords, indexing='ij')
            rho = jnp.sqrt(xx * xx + yy * yy)
            theta = jnp.arctan2(yy, xx)
            K = finsler_params.shape[-1]
            B = _harmonic_basis(theta, K)
            g = jnp.einsum('ck,ijk->cij', finsler_params, B)
            e = 2.0 * alpha / (2.0 * alpha - 1.0)
            nu = (2.0 * alpha - 1.0) * (2.0 * alpha) ** (-e)
            return nu * (rho ** e)[None, :, :] * jnp.exp(-e * g)

        def dilation(u, kernel, r):
            Bn, C, H, W = u.shape
            ks = 2 * r + 1
            pad = jnp.pad(u, ((0, 0), (0, 0), (r, r), (r, r)), constant_values=NEG)
            kflat = kernel.reshape(C, ks * ks)

            def body(acc, idx):
                di = idx // ks
                dj = idx % ks
                sl = jax.lax.dynamic_slice(pad, (0, 0, di, dj), (Bn, C, H, W))
                acc = jnp.maximum(acc, sl - kflat[:, idx][None, :, None, None])
                return (acc, None)
            acc0 = jnp.full((Bn, C, H, W), NEG, dtype=u.dtype)
            acc, _ = jax.lax.scan(body, acc0, jnp.arange(ks * ks))
            return acc
        key = jax.random.key(seed)
        k1, k2 = jax.random.split(key)
        inp = jax.random.normal(k1, (8, 32, 256, 256), dtype=jnp.float32)
        fp = jax.random.uniform(k2, (32, 6), dtype=jnp.float32, minval=-0.5, maxval=0.5)
        return {'input': inp, 'finsler_params': fp}
    _L0_conv_all = _L0_conv_setup()
    _L0_conv_in = {k: v for k, v in _L0_conv_all.items() if k in ('finsler_params',)}
    del _L0_conv_all

    def _L1_conv_setup():
        import jax, jax.numpy as jnp
        import numpy as np
        B, C, H, W, K = (16, 32, 128, 128, 3)
        OFFSET_RANGE_FACTOR = 1.0
        BN_EPS = 1e-05

        def _grid_sample_bilinear(img, grid):
            Bq, Cq, Hq, Wq = img.shape
            gx = (grid[..., 0] + 1.0) * 0.5 * (Wq - 1)
            gy = (grid[..., 1] + 1.0) * 0.5 * (Hq - 1)
            x0 = jnp.floor(gx)
            y0 = jnp.floor(gy)
            wx1 = gx - x0
            wy1 = gy - y0

            def corner(yi, xi, w):
                yc = jnp.clip(yi, 0, Hq - 1).astype(jnp.int32)
                xc = jnp.clip(xi, 0, Wq - 1).astype(jnp.int32)
                valid = (yi >= 0) & (yi <= Hq - 1) & (xi >= 0) & (xi <= Wq - 1)
                v = jax.vmap(lambda im, y, x: im[:, y, x])(img, yc, xc)
                return v * (w * valid.astype(img.dtype))[:, None, :, :]
            return corner(y0, x0, (1 - wy1) * (1 - wx1)) + corner(y0, x0 + 1, (1 - wy1) * wx1) + corner(y0 + 1, x0, wy1 * (1 - wx1)) + corner(y0 + 1, x0 + 1, wy1 * wx1)
        key = jax.random.key(seed)
        ks = jax.random.split(key, 5)
        s = lambda k, shp: jax.random.normal(k, shp, jnp.float32) * 0.1
        return dict(x=jax.random.normal(ks[0], (B, C, H, W), jnp.float32), proj_w=s(ks[1], (C, C, 1, 1)), proj_b=jnp.zeros((C,), jnp.float32), dw_w=s(ks[2], (C, 1, K, K)), dw_b=jnp.zeros((C,), jnp.float32), bn_g=jnp.ones((C,), jnp.float32), bn_b=jnp.zeros((C,), jnp.float32), off_w=s(ks[3], (2, C, 1, 1)))
    _L1_conv_all = _L1_conv_setup()
    _L1_conv_in = {k: v for k, v in _L1_conv_all.items() if k in ('proj_w', 'proj_b', 'dw_w', 'dw_b', 'bn_g', 'bn_b', 'off_w')}
    del _L1_conv_all
    return {'x': x, 'L0_conv_finsler_params': _L0_conv_in['finsler_params'], 'L1_conv_proj_w': _L1_conv_in['proj_w'], 'L1_conv_proj_b': _L1_conv_in['proj_b'], 'L1_conv_dw_w': _L1_conv_in['dw_w'], 'L1_conv_dw_b': _L1_conv_in['dw_b'], 'L1_conv_bn_g': _L1_conv_in['bn_g'], 'L1_conv_bn_b': _L1_conv_in['bn_b'], 'L1_conv_off_w': _L1_conv_in['off_w']}

def reference(x, L0_conv_finsler_params, L1_conv_proj_w, L1_conv_proj_b, L1_conv_dw_w, L1_conv_dw_b, L1_conv_bn_g, L1_conv_bn_b, L1_conv_off_w):
    import jax
    import jax.numpy as jnp

    def _L0_conv_ref(input, finsler_params):
        import jax, jax.numpy as jnp
        import numpy as np
        R = 5
        ALPHA = 0.65
        NEG = -1e+30

        def _harmonic_basis(theta, K):
            feats = []
            for k in range(1, K + 1):
                m = (k + 1) // 2
                feats.append(jnp.cos(m * theta) if k % 2 == 1 else jnp.sin(m * theta))
            return jnp.stack(feats, axis=-1)

        def morphological_kernel(finsler_params, r, alpha):
            coords = jnp.arange(-r, r + 1, dtype=jnp.float32)
            yy, xx = jnp.meshgrid(coords, coords, indexing='ij')
            rho = jnp.sqrt(xx * xx + yy * yy)
            theta = jnp.arctan2(yy, xx)
            K = finsler_params.shape[-1]
            B = _harmonic_basis(theta, K)
            g = jnp.einsum('ck,ijk->cij', finsler_params, B)
            e = 2.0 * alpha / (2.0 * alpha - 1.0)
            nu = (2.0 * alpha - 1.0) * (2.0 * alpha) ** (-e)
            return nu * (rho ** e)[None, :, :] * jnp.exp(-e * g)

        def dilation(u, kernel, r):
            Bn, C, H, W = u.shape
            ks = 2 * r + 1
            pad = jnp.pad(u, ((0, 0), (0, 0), (r, r), (r, r)), constant_values=NEG)
            kflat = kernel.reshape(C, ks * ks)

            def body(acc, idx):
                di = idx // ks
                dj = idx % ks
                sl = jax.lax.dynamic_slice(pad, (0, 0, di, dj), (Bn, C, H, W))
                acc = jnp.maximum(acc, sl - kflat[:, idx][None, :, None, None])
                return (acc, None)
            acc0 = jnp.full((Bn, C, H, W), NEG, dtype=u.dtype)
            acc, _ = jax.lax.scan(body, acc0, jnp.arange(ks * ks))
            return acc
        kernel = morphological_kernel(finsler_params, R, ALPHA)
        return dilation(input, kernel, R)

    def _L1_conv_ref(x, proj_w, proj_b, dw_w, dw_b, bn_g, bn_b, off_w):
        import jax, jax.numpy as jnp
        import numpy as np
        B, C, H, W, K = (16, 32, 128, 128, 3)
        OFFSET_RANGE_FACTOR = 1.0
        BN_EPS = 1e-05

        def _grid_sample_bilinear(img, grid):
            Bq, Cq, Hq, Wq = img.shape
            gx = (grid[..., 0] + 1.0) * 0.5 * (Wq - 1)
            gy = (grid[..., 1] + 1.0) * 0.5 * (Hq - 1)
            x0 = jnp.floor(gx)
            y0 = jnp.floor(gy)
            wx1 = gx - x0
            wy1 = gy - y0

            def corner(yi, xi, w):
                yc = jnp.clip(yi, 0, Hq - 1).astype(jnp.int32)
                xc = jnp.clip(xi, 0, Wq - 1).astype(jnp.int32)
                valid = (yi >= 0) & (yi <= Hq - 1) & (xi >= 0) & (xi <= Wq - 1)
                v = jax.vmap(lambda im, y, x: im[:, y, x])(img, yc, xc)
                return v * (w * valid.astype(img.dtype))[:, None, :, :]
            return corner(y0, x0, (1 - wy1) * (1 - wx1)) + corner(y0, x0 + 1, (1 - wy1) * wx1) + corner(y0 + 1, x0, wy1 * (1 - wx1)) + corner(y0 + 1, x0 + 1, wy1 * wx1)
        out = jnp.einsum('oi,bihw->bohw', proj_w[:, :, 0, 0], x) + proj_b[None, :, None, None]
        h = jax.lax.conv_general_dilated(out, dw_w, window_strides=(1, 1), padding=((1, 1), (1, 1)), feature_group_count=C, dimension_numbers=('NCHW', 'OIHW', 'NCHW'))
        h = h + dw_b[None, :, None, None]
        mean = h.mean(axis=(0, 2, 3))
        var = h.var(axis=(0, 2, 3))
        h = (h - mean[None, :, None, None]) * jax.lax.rsqrt(var + BN_EPS)[None, :, None, None]
        h = h * bn_g[None, :, None, None] + bn_b[None, :, None, None]
        h = jax.nn.gelu(h, approximate=False)
        offset = jnp.einsum('oc,bchw->bohw', off_w[:, :, 0, 0], h)
        Hk, Wk = (offset.shape[2], offset.shape[3])
        rng = jnp.array([1.0 / (Hk - 1.0), 1.0 / (Wk - 1.0)], jnp.float32)
        offset = jnp.tanh(offset) * rng[None, :, None, None] * OFFSET_RANGE_FACTOR
        offset = jnp.transpose(offset, (0, 2, 3, 1))
        ry = jnp.linspace(0.5, Hk - 0.5, Hk, dtype=jnp.float32) / (Hk - 1.0) * 2.0 - 1.0
        rx = jnp.linspace(0.5, Wk - 0.5, Wk, dtype=jnp.float32) / (Wk - 1.0) * 2.0 - 1.0
        ref = jnp.stack(jnp.meshgrid(ry, rx, indexing='ij'), axis=-1)
        pos = offset + ref[None]
        grid = pos[..., ::-1]
        return _grid_sample_bilinear(x, grid)

    def _gn(v, G=16, eps=1e-05):
        B_, C_, H_, W_ = v.shape
        g = v.reshape(B_, G, C_ // G, H_, W_)
        m = jnp.mean(g, axis=(2, 3, 4), keepdims=True)
        s = jnp.var(g, axis=(2, 3, 4), keepdims=True)
        return ((g - m) / jnp.sqrt(s + eps)).reshape(v.shape)

    def _ln_c(v, eps=1e-06):
        m = jnp.mean(v, axis=1, keepdims=True)
        s = jnp.var(v, axis=1, keepdims=True)
        return (v - m) / jnp.sqrt(s + eps)

    def _ln_t(v, eps=1e-05):
        m = jnp.mean(v, axis=-1, keepdims=True)
        s = jnp.var(v, axis=-1, keepdims=True)
        return (v - m) / jnp.sqrt(s + eps)

    def _to_tokens(v):
        B_, C_, H_, W_ = v.shape
        return v.reshape(B_, C_, H_ * W_).transpose(0, 2, 1)

    def _from_tokens(t, like):
        B_, C_, H_, W_ = like.shape
        return t.transpose(0, 2, 1).reshape(B_, C_, H_, W_)
    x = x + _L0_conv_ref(_gn(x), L0_conv_finsler_params)
    x = x + _L1_conv_ref(_gn(x), L1_conv_proj_w, L1_conv_proj_b, L1_conv_dw_w, L1_conv_dw_b, L1_conv_bn_g, L1_conv_bn_b, L1_conv_off_w)
    return x

_drawn_inputs = setup_inputs


def setup_inputs(seed=0):
    import zlib

    import numpy as np

    out = dict(_drawn_inputs(seed))
    spreads = {'L1_conv_proj_b': (0.0, 0.8),
     'L1_conv_dw_b': (0.0, 0.8),
     'L1_conv_bn_g': (1.0, 0.2),
     'L1_conv_bn_b': (0.0, 0.799)}
    factors = {}
    for name, (base, spread) in spreads.items():
        noise = np.random.default_rng([zlib.crc32(name.encode()), seed]).standard_normal(out[name].shape)
        drawn = base * np.exp(spread * noise) if base else spread * noise
        out[name] = jnp.asarray(drawn.astype(out[name].dtype))
    for name, factor in factors.items():
        out[name] = (out[name] * factor).astype(out[name].dtype)
    return out
```

```python
from contextlib import ExitStack

import concourse.bass as bass
import numpy as np
from concourse import mybir

F32 = mybir.dt.float32
ALU = mybir.AluOpType
ACT = mybir.ActivationFunctionType
DVE_ONLY = [mybir.EngineType.DVE]
ACT_ONLY = [mybir.EngineType.Activation]
PE_ONLY = [mybir.EngineType.PE]
POOL_ONLY = [mybir.EngineType.Pool]
SP_ONLY = [mybir.EngineType.SP]

P = 128
CH = 32
IMG = P // CH
H = W = 256
GROUPS = 8 // IMG
R = 5
KS = 2 * R + 1
WR = 16
WIN = H // WR
NWIN = GROUPS * WIN
UR, UC = WR + 2 * R, W + 2 * R
CR = 8
CPW = WR // CR
HALF = CR // 2 * W
NEG = -1e30
GN_EPS = 1e-5
BN_EPS = 1e-5
ALPHA = 0.65
EXPO = 2.0 * ALPHA / (2.0 * ALPHA - 1.0)
NU = (2.0 * ALPHA - 1.0) * (2.0 * ALPHA) ** (-EXPO)
BANK = 512
TAPS_PE = 3

COL_FP, COL_PB, COL_DW, COL_DB, COL_BG, COL_BB, COL_OFF, COL_END = 0, 6, 7, 16, 17, 18, 19, 21


def passed(engine, turns):
    engine.sem_inc(turns, 1)


def dilation_plan(pool_pairs, pe_pairs):
    pairs = []
    for di in range(KS):
        for base, outer in ((5, 6), (7, 8), (9, 10), (4, 3), (2, 1)):
            pairs.append((di, base, outer))
    singles = [(di, 0) for di in range(KS)]
    while len(pairs) > pool_pairs + pe_pairs:
        di, base, outer = pairs.pop()
        singles += [(di, base), (di, outer)]
    return pairs, singles


def shape_constants():
    coords = np.arange(-R, R + 1, dtype=np.float32)
    yy, xx = np.meshgrid(coords, coords, indexing="ij")
    rho = np.sqrt(xx * xx + yy * yy)
    theta = np.arctan2(yy, xx)
    basis = []
    for k in range(1, 7):
        m = (k + 1) // 2
        basis.append(np.cos(m * theta) if k % 2 == 1 else np.sin(m * theta))
    radial = (np.float32(NU) * rho ** np.float32(EXPO)).astype(np.float32)
    rows = np.stack(basis + [radial]).astype(np.float32).reshape(1, 7 * KS * KS)
    p = np.arange(P)
    ident = np.eye(P, dtype=np.float32)
    pair_mean = (p[:, None] // 2 == p[None, :] // 2).astype(np.float32) * np.float32(0.5)
    channel_mean = (p[:, None] % CH == p[None, :] % CH).astype(np.float32) * np.float32(1.0 / IMG)
    same_image = (p[:, None] // CH == p[None, :] // CH).astype(np.float32)
    return np.repeat(rows, P, 0), np.stack([ident, pair_mean, channel_mean, same_image], 1).copy()


def build(nc, x, params, proj_w, basis_in, mats_in, out):
    x_pl = x.rearrange("b c h w -> (b c) (h w)")
    out_pl = out.rearrange("b c h w -> (b c) (h w)")
    x1_pl = nc.dram_tensor("x1_scratch", (GROUPS * P, H * W), F32, kind="Internal").ap()
    h_pl = nc.dram_tensor("h_scratch", (GROUPS * P, H * W), F32, kind="Internal").ap()

    with ExitStack() as ctx:
        def sb(name, shape):
            return ctx.enter_context(nc.sbuf_tensor(name, shape, F32))

        mats = sb("mats", [P, 4, P])
        par = sb("par", [P, COL_END])
        kt = sb("kt", [P, KS * KS])
        nkt = sb("nkt", [P, KS * KS])
        gap_r = sb("gap_r", [P, KS * KS])
        gap_l = sb("gap_l", [P, KS * KS])
        norm1 = sb("norm1", [P, 2, 3, NWIN + 1])
        shift1 = sb("shift1", [P, NWIN + 1])
        sums1 = sb("sums1", [P, 2, NWIN * CPW + 1])
        eps = sb("eps", [P, 1])
        small = sb("small", [P, 64])
        ident = mats[:, 0, :]
        pair_mean = mats[:, 1, :]
        channel_mean = mats[:, 2, :]
        same_image = mats[:, 3, :]

        stats_and_tables(nc, x_pl, params, basis_in, mats_in, mats, par, kt, nkt, gap_r, gap_l,
                         norm1, shift1, eps, small, pair_mean)
        dilation(nc, x_pl, x1_pl, ident, kt, nkt, gap_r, gap_l, norm1, shift1, sums1)
        conv_in = sb("conv_in", [P, GROUPS, 2])
        h_shift = sb("h_shift", [P, 1])
        h_sums = sb("h_sums", [P, 2, NWIN + 1])
        convolution(nc, x1_pl, h_pl, proj_w, mats, par, shift1, sums1, eps, conv_in, h_shift, h_sums)
        resample(nc, x1_pl, h_pl, out_pl, mats, par, eps, conv_in, h_shift, h_sums)
    return nc


def stats_and_tables(nc, x_pl, params, basis_in, mats_in, mats, par, kt, nkt, gap_r, gap_l,
                     norm1, shift1, eps, small, pair_mean):
    TILE = 4096
    SLOTS = 4
    TILES = H * W // TILE
    SUB = TILE // BANK
    with ExitStack() as ctx:
        xt = ctx.enter_context(nc.sbuf_tensor("xt", [P, SLOTS, TILE], F32))
        stats = ctx.enter_context(nc.sbuf_tensor("stats", [P, GROUPS, TILES * SUB * 6], F32))
        bas = ctx.enter_context(nc.sbuf_tensor("bas", [P, 7, KS * KS], F32))
        ang = ctx.enter_context(nc.sbuf_tensor("ang", [P, KS * KS], F32))
        pstat = ctx.enter_context(nc.psum_tensor("pstat", [P, BANK], F32))
        consts_loaded = ctx.enter_context(nc.semaphore("consts_loaded"))
        tile_loaded = [ctx.enter_context(nc.semaphore(f"tile_loaded{s}")) for s in range(SLOTS)]
        tile_used = ctx.enter_context(nc.semaphore("tile_used"))
        sp_turns = ctx.enter_context(nc.semaphore("sp_turns1"))
        step = ctx.enter_context(nc.semaphore("step"))
        angle_ready = ctx.enter_context(nc.semaphore("angle_ready"))
        exp_ready = ctx.enter_context(nc.semaphore("exp_ready"))
        moments_ready = ctx.enter_context(nc.semaphore("moments_ready"))
        means_ready = ctx.enter_context(nc.semaphore("means_ready"))
        var_ready = ctx.enter_context(nc.semaphore("var_ready"))
        std_ready = ctx.enter_context(nc.semaphore("std_ready"))
        mv = small[:, 0:4].rearrange("p (g t) -> p g t", t=2)
        mom = small[:, 4:8].rearrange("p (g t) -> p g t", t=2)
        var = small[:, 8:10]
        rstd = small[:, 10:12]
        nbias = small[:, 12:14]
        gm = small[:, 14:18].rearrange("p (g t) -> p g t", t=2)

        with nc.Block() as block:
            @block.sync
            def _(sp):
                sp.dma_start(bas[:].rearrange("p k n -> p (k n)"), basis_in).then_inc(consts_loaded, 16)
                sp.dma_start(par[:], params).then_inc(consts_loaded, 16)
                sp.dma_start(mats[:], mats_in).then_inc(consts_loaded, 16)
                for g in range(GROUPS):
                    src = x_pl[g * P:(g + 1) * P, :]
                    for s in range(SLOTS):
                        t = g * TILES + s
                        if g > 0:
                            sp.wait_ge(tile_used, t - SLOTS + 1)
                        sp.dma_start(xt[:, s, :], src[:, s * TILE:(s + 1) * TILE]).then_inc(tile_loaded[s], 16)
                    with nc.Fori(1, TILES // SLOTS, engines=SP_ONLY) as i:
                        for s in range(SLOTS):
                            sp.wait_ge(tile_used, i * SLOTS + (g * TILES + s + 1 - SLOTS))
                            passed(sp, sp_turns)
                            sp.dma_start(xt[:, s, :], src[:, bass.ds(i * (SLOTS * TILE) + s * TILE, TILE)]) \
                                .then_inc(tile_loaded[s], 16)

            @block.vector
            def _(dve):
                steps = [0]

                def link(ins):
                    steps[0] += 1
                    ins.then_inc(step, 1)
                    dve.wait_ge(step, steps[0])

                link(nc.vector.memset(eps[:], GN_EPS))
                dve.wait_ge(consts_loaded, 48)
                link(nc.vector.tensor_scalar(ang[:], bas[:, 0, :], par[:, COL_FP:COL_FP + 1], None, ALU.mult))
                for k in range(1, 6):
                    link(nc.vector.scalar_tensor_tensor(out=ang[:], in0=bas[:, k, :],
                                                        scalar=par[:, COL_FP + k:COL_FP + k + 1],
                                                        in1=ang[:], op0=ALU.mult, op1=ALU.add))
                nc.vector.sem_inc(angle_ready, 1)
                dve.wait_ge(exp_ready, 1)
                link(nc.vector.tensor_tensor(kt[:], ang[:], bas[:, 6, :], ALU.mult))
                link(nc.vector.tensor_scalar(nkt[:], kt[:], -1.0, None, ALU.mult))
                link(nc.vector.memset(gap_r[:], 0.0))
                link(nc.vector.memset(gap_l[:], 0.0))
                n = KS * KS
                link(nc.vector.tensor_tensor(gap_r[:, 0:n - 1], kt[:, 0:n - 1], kt[:, 1:n], ALU.subtract))
                link(nc.vector.tensor_tensor(gap_l[:, 1:n], kt[:, 1:n], kt[:, 0:n - 1], ALU.subtract))
                for g in range(GROUPS):
                    with nc.Fori(0, TILES // SLOTS, engines=DVE_ONLY) as i:
                        for s in range(SLOTS):
                            dve.wait_ge(tile_loaded[s], i * 16 + (g * (TILES // SLOTS) + 1) * 16)
                            for j in range(SUB):
                                at = i * (SLOTS * SUB * 6) + (s * SUB + j) * 6
                                last = nc.vector.bn_stats(stats[:, g, bass.ds(at, 6)],
                                                          xt[:, s, j * BANK:(j + 1) * BANK])
                            last.then_inc(tile_used, 1)
                dve.wait_ge(tile_used, GROUPS * TILES)
                for g in range(GROUPS):
                    link(nc.vector.bn_aggr(mv[:, g, :], stats[:, g, :]))
                link(nc.vector.tensor_tensor(mom[:, :, 1], mv[:, :, 0], mv[:, :, 0], ALU.mult))
                link(nc.vector.tensor_tensor(mom[:, :, 1], mom[:, :, 1], mv[:, :, 1], ALU.add))
                nc.vector.tensor_copy(mom[:, :, 0], mv[:, :, 0]).then_inc(moments_ready, 1)
                dve.wait_ge(means_ready, 1)
                link(nc.vector.tensor_copy(gm, pstat[:, 0:4].rearrange("p (g t) -> p g t", t=2)))
                link(nc.vector.tensor_tensor(var, gm[:, :, 0], gm[:, :, 0], ALU.mult))
                nc.vector.tensor_tensor(var, gm[:, :, 1], var, ALU.subtract).then_inc(var_ready, 1)
                dve.wait_ge(std_ready, 1)
                link(nc.vector.reciprocal(rstd, rstd))
                link(nc.vector.scalar_tensor_tensor(out=nbias, in0=gm[:, :, 0], scalar=-1.0, in1=rstd,
                                                    op0=ALU.mult, op1=ALU.mult))
                link(nc.vector.memset(norm1[:], 1.0))
                link(nc.vector.memset(shift1[:], 1.0))
                for g in range(GROUPS):
                    lo, hi = g * WIN, (g + 1) * WIN + (g == GROUPS - 1)
                    link(nc.vector.tensor_scalar(norm1[:, 0, :, lo:hi], norm1[:, 0, :, lo:hi],
                                                 rstd[:, g:g + 1], None, ALU.mult))
                    link(nc.vector.tensor_scalar(norm1[:, 1, :, lo:hi], norm1[:, 1, :, lo:hi],
                                                 nbias[:, g:g + 1], None, ALU.mult))
                    link(nc.vector.tensor_scalar(shift1[:, lo + 1:lo + WIN + 1], shift1[:, lo + 1:lo + WIN + 1],
                                                 gm[:, g, 0:1], -1.0, ALU.mult, ALU.mult))
                    for kind, w in ((0, lo), (2, lo + WIN - 1)):
                        link(nc.vector.memset(norm1[:, 0, kind, w:w + 1], 0.0))
                        link(nc.vector.memset(norm1[:, 1, kind, w:w + 1], NEG))

            @block.scalar
            def _(act):
                act.wait_ge(angle_ready, 1)
                act.wait_ge(step, 7)
                nc.scalar.activation(ang[:], ang[:], ACT.Exp, scale=-EXPO).then_inc(exp_ready, 1)
                act.wait_ge(var_ready, 1)
                nc.scalar.activation(rstd, var, ACT.Sqrt, bias=eps[:, 0:1]).then_inc(std_ready, 1)

            @block.tensor
            def _(pe):
                pe.wait_ge(moments_ready, 1)
                pe.wait_ge(consts_loaded, 48)
                nc.tensor.matmul(pstat[:, 0:4], pair_mean, small[:, 4:8], start=True, stop=True) \
                    .then_inc(means_ready, 1)


def dilation(nc, x_pl, x1_pl, ident, kt, nkt, gap_r, gap_l, norm1, shift1, sums1):
    NPOOL, NPE = 32, 22
    NORM_PIECES = ((0, 0, R), (1, R, R + WR // 2), (1, R + WR // 2, R + WR), (2, R + WR, UR))
    NORM_TURNS = (16, 20, 24, 28)
    DX_PIECES = ((0, 5), (5, 9), (9, 13), (13, 17), (17, 21), (21, UR))
    DX_AT = ((0, 22), (0, 26), (0, 30), (1, 4), (1, 9), (1, 14))
    NU, ND = len(NORM_PIECES), len(DX_PIECES)
    START_TURN, SUMS_TURN = 4, 9
    pairs, singles = dilation_plan(NPOOL, NPE)
    NCHUNK = NWIN * CPW
    CH_IT = 2 * CPW
    pool_pairs, pe_pairs = [], []
    for n, pair in enumerate(pairs):
        (pool_pairs if len(pool_pairs) * NPE <= len(pe_pairs) * NPOOL and len(pool_pairs) < NPOOL
         or len(pe_pairs) >= NPE else pe_pairs).append(pair)
    init_a, init_b, *rest = singles
    order = [((j + 0.8) / NPOOL, "pool", j) for j in range(NPOOL)]
    order += [((h + 0.9) / (2 * NPE), "pe", h) for h in range(2 * NPE)]
    order += [((j + 0.7) / len(rest), "single", j) for j in range(len(rest))]
    order = [(kind, j) for _, kind, j in sorted(order)]
    act_order = [((j + 0.5) / NPOOL, "pool", j) for j in range(NPOOL)]
    act_order += [((j + 0.3) / NPE, "pe", j) for j in range(NPE)]
    act_order = [(kind, j) for _, kind, j in sorted(act_order)]
    head = [("pe", 0), ("pool", 0), ("pool", 1), ("pe", 1)]
    act_order = head + [x for x in act_order if x not in head]

    NA = sum(kind != "pe" for kind, _ in order)
    NB = 2 * NPE
    a_before = {}
    count = 0
    for kind, j in order:
        count += kind != "pe"
        if kind == "pool":
            a_before[j] = count

    def col(di, dj):
        return di * KS + dj

    with ExitStack() as ctx:
        def sb(name, shape):
            return ctx.enter_context(nc.sbuf_tensor(name, shape, F32))

        def sem(name):
            return ctx.enter_context(nc.semaphore(name))

        u = [sb(f"u{s}", [P, UR, UC]) for s in range(2)]
        dx = [sb(f"dx{s}", [P, UR, UC]) for s in range(2)]
        r_pool = [sb(f"r_pool{s}", [P, CR, W]) for s in range(2)]
        r_pe = [sb(f"r_pe{s}", [P, CR, W]) for s in range(2)]
        m_pool = [sb(f"m_pool{s}", [P, CR, W]) for s in range(2)]
        acc_b = sb("acc_b", [P, CR, W])
        xc = [sb(f"xc{s}", [P, CR, W]) for s in range(2)]
        x1 = [sb(f"x1{s}", [P, CR, W]) for s in range(2)]
        acc_a = ctx.enter_context(nc.psum_tensor("acc_a", [P, CR, W], F32))
        m_pe = [ctx.enter_context(nc.psum_tensor(f"m_pe{s}", [P, CR // 2, W], F32)) for s in range(2)]

        pads_set = sem("pads_set")
        win_loaded = [sem(f"win_loaded{s}") for s in range(2)]
        xc_loaded = [sem(f"xc_loaded{k}") for k in range(CPW)]
        x1_stored = [sem(f"x1_stored{k}") for k in range(CPW)]
        u_ready = sem("u_ready")
        dx_ready = sem("dx_ready")
        r_pool_ready = sem("r_pool_ready")
        r_pe_ready = sem("r_pe_ready")
        m_pool_ready = sem("m_pool_ready")
        m_pe_ready = sem("m_pe_ready")
        a_started = sem("a_started")
        b_started = sem("b_started")
        a_done = sem("a_done")
        b_done = sem("b_done")
        joined = sem("joined")
        chunk_done = sem("chunk_done")
        x1_summed = sem("x1_summed")
        act_turns, sp_turns = sem("act_turns"), sem("sp_turns")

        def at(c, per_chunk, count):
            return c * per_chunk + (per_chunk + count)

        with nc.Block() as block:
            @block.sync
            def _(sp):
                def load_window(slot, w, g, top=False, bottom=False):
                    lo, n = (R, WR + R) if top else (0, WR + R if bottom else UR)
                    first = w * (WR * W) + (0 if top else -R * W)
                    sp.dma_start(u[slot][:, lo:lo + n, R:R + W],
                                 x_pl[g * P:(g + 1) * P, bass.ds(first, n * W)]
                                 .rearrange("p (r w) -> p r w", w=W)).then_inc(win_loaded[slot], 16)

                def load_chunk(w, k, g):
                    sp.dma_start(xc[k][:].rearrange("p r w -> p (r w)"),
                                 x_pl[g * P:(g + 1) * P, bass.ds(w * (WR * W) + k * (CR * W), CR * W)]) \
                        .then_inc(xc_loaded[k], 16)

                def window(n, w, slot, g, ahead_w, ahead_g, top=False, bottom=False):
                    for k in range(CPW):
                        sp.wait_ge(chunk_done, n * CPW + (CPW + k + 1))
                        passed(sp, sp_turns)
                        sp.dma_start(x1_pl[g * P:(g + 1) * P, bass.ds(w * (WR * W) + k * (CR * W), CR * W)],
                                     x1[k][:].rearrange("p r w -> p (r w)")).then_inc(x1_stored[k], 16)
                        if k == CPW - 1 and ahead_w is not None:
                            load_window(slot, ahead_w, ahead_g, top, bottom)
                        if isinstance(n, int) and n == NWIN - 1:
                            continue
                        sp.wait_ge(x1_summed, n * (2 * CPW) + (2 * k + 4))
                        passed(sp, sp_turns)
                        last = isinstance(w, int) and w == WIN - 1
                        load_chunk(0 if last else w + 1, k, g + 1 if last else g)

                sp.sem_inc(x1_stored[0], 16)
                sp.sem_inc(x1_stored[1], 16)
                sp.wait_ge(pads_set, 1)
                load_window(0, 0, 0, top=True)
                load_window(1, 1, 0)
                load_chunk(0, 0, 0)
                sp.wait_ge(x1_summed, 2)
                load_chunk(0, 1, 0)
                for g in range(GROUPS):
                    base = g * WIN
                    with nc.Fori(0, (WIN - 4) // 2, engines=SP_ONLY) as i:
                        for s in range(2):
                            w = i * 2 + s
                            window(w + base, w, s, g, w + 2, g)
                    ahead = min(g + 1, GROUPS - 1)
                    window(base + WIN - 4, WIN - 4, 0, g, WIN - 2, g)
                    window(base + WIN - 3, WIN - 3, 1, g, WIN - 1, g, bottom=True)
                    window(base + WIN - 2, WIN - 2, 0, g, 0, ahead, top=True)
                    window(base + WIN - 1, WIN - 1, 1, g, 1 if g + 1 < GROUPS else None, ahead)
                for s in range(2):
                    sp.wait_ge(win_loaded[s], (NWIN // 2 + 1 - s) * 16)
                    sp.wait_ge(xc_loaded[s], NWIN * 16)
                    sp.wait_ge(x1_stored[s], (NWIN + 1) * 16)

            @block.gpsimd
            def _(pool):
                def difference(n, slot, piece):
                    if piece == 0:
                        pool.wait_ge(u_ready, n * NU + NU)
                    lo, hi = DX_PIECES[piece]
                    nc.gpsimd.tensor_tensor(dx[slot][:, lo:hi, 0:UC - 1], u[slot][:, lo:hi, 1:UC],
                                            u[slot][:, lo:hi, 0:UC - 1], ALU.subtract).then_inc(dx_ready, 1)

                pool.sem_inc(m_pool_ready, NPOOL)
                pool.wait_ge(pads_set, 1)
                for piece in range(ND):
                    difference(0, 0, piece)
                with nc.Fori(0, NWIN // 2, engines=POOL_ONLY) as i:
                    for s in range(2):
                        for k in range(CPW):
                            c = i * CH_IT + (s * CPW + k)
                            for j, (di, base, outer) in enumerate(pool_pairs):
                                pool.wait_ge(r_pool_ready, at(c, NPOOL, j + 1))
                                used = a_before[j - 2] if j >= 2 else a_before[NPOOL + j - 2] - NA
                                pool.wait_ge(a_done, at(c, NA, used))
                                nc.gpsimd.tensor_tensor(
                                    m_pool[j % 2][:], r_pool[j % 2][:],
                                    u[s][:, k * CR + di:k * CR + di + CR, base:base + W],
                                    ALU.add).then_inc(m_pool_ready, 1)
                                if (k, j) in DX_AT:
                                    difference(i * 2 + (s + 1), 1 - s, DX_AT.index((k, j)))

            @block.tensor
            def _(pe):
                pe.sem_inc(m_pe_ready, NB)
                with nc.Fori(0, NWIN // 2, engines=PE_ONLY) as i:
                    for s in range(2):
                        for k in range(CPW):
                            c = i * CH_IT + (s * CPW + k)
                            for j, (di, base, outer) in enumerate(pe_pairs):
                                pe.wait_ge(r_pe_ready, at(c, NPE, j + 1))
                                for half in range(2):
                                    pe.wait_ge(b_done, at(c, NB, 2 * j + half - 1))
                                    for q in range(2):
                                        row = (half * 2 + q) * 2
                                        dst = m_pe[half][:, 2 * q:2 * q + 2, :]
                                        top = k * CR + di + row
                                        nc.tensor.matmul(dst, ident, u[s][:, top:top + 2, base:base + W],
                                                         start=True, stop=False)
                                        last = nc.tensor.matmul(dst, ident, r_pe[j % 2][:, row:row + 2, :],
                                                                start=False, stop=True)
                                    last.then_inc(m_pe_ready, 1)

            @block.scalar
            def _(act):
                def normalise(n, slot, loads, piece):
                    if piece == 0:
                        act.wait_ge(win_loaded[slot], loads * 16)
                        passed(act, act_turns)
                    kind, lo, hi = NORM_PIECES[piece]
                    rows = u[slot][:, lo:hi, R:R + W]
                    nc.scalar.activation(rows, rows, ACT.Identity,
                                         bias=norm1[:, 1, kind, bass.ds(n, 1)],
                                         scale=norm1[:, 0, kind, bass.ds(n, 1)]).then_inc(u_ready, 1)

                def start(acc, offset, s, k, started):
                    di, dj = offset
                    nc.scalar.activation(acc[:], u[s][:, k * CR + di:k * CR + di + CR, dj:dj + W], ACT.Identity,
                                         bias=nkt[:, col(di, dj):col(di, dj) + 1]).then_inc(started, 1)

                def sums_before(c, k, shift_column):
                    act.wait_ge(chunk_done, c + CPW)
                    passed(act, act_turns)
                    shift = shift1[:, bass.ds(shift_column, 1)]
                    nc.scalar.activation(xc[1 - k][:], x1[1 - k][:], ACT.Identity, bias=shift,
                                         accum_out=sums1[:, 0, bass.ds(c, 1)]).then_inc(x1_summed, 1)
                    act.wait_ge(x1_summed, c * 2 + 1)
                    passed(act, act_turns)
                    nc.scalar.activation(xc[1 - k][:], x1[1 - k][:], ACT.Square, bias=shift,
                                         accum_out=sums1[:, 1, bass.ds(c, 1)]).then_inc(x1_summed, 1)

                act.sem_inc(r_pool_ready, NPOOL)
                act.sem_inc(r_pe_ready, NPE)
                act.wait_ge(pads_set, 1)
                for piece in range(NU):
                    normalise(0, 0, 1, piece)
                with nc.Fori(0, NWIN // 2, engines=ACT_ONLY) as i:
                    for s in range(2):
                        n = i * 2 + s
                        for k in range(CPW):
                            c = i * CH_IT + (s * CPW + k)
                            if k == 0:
                                act.wait_ge(u_ready, n * NU + NU)
                                act.wait_ge(dx_ready, n * ND + ND)
                            for turn, (kind, j) in enumerate(act_order):
                                if turn == START_TURN:
                                    act.wait_ge(joined, at(c, 1, 0))
                                    start(acc_b, init_b, s, k, b_started)
                                    act.wait_ge(chunk_done, c + CPW)
                                    start(acc_a, init_a, s, k, a_started)
                                if turn == SUMS_TURN:
                                    sums_before(c, k, n + k)
                                if kind == "pool":
                                    di, base, outer = pool_pairs[j]
                                    dst, ready = r_pool[j % 2], r_pool_ready
                                    act.wait_ge(m_pool_ready, at(c, NPOOL, j - 1))
                                else:
                                    di, base, outer = pe_pairs[j]
                                    dst, ready = r_pe[j % 2], r_pe_ready
                                    act.wait_ge(m_pe_ready, at(c, NB, 2 * (j - 1)))
                                right = outer > base
                                lo = base if right else outer
                                gap = gap_r if right else gap_l
                                nc.scalar.activation(
                                    dst[:], dx[s][:, k * CR + di:k * CR + di + CR, lo:lo + W], ACT.Relu,
                                    bias=gap[:, col(di, base):col(di, base) + 1],
                                    scale=1.0 if right else -1.0).then_inc(ready, 1)
                                if k == 0 and turn in NORM_TURNS:
                                    normalise(n + 1, 1 - s, i + (1 + s), NORM_TURNS.index(turn))
                sums_before(NCHUNK, 0, NWIN)

            @block.vector
            def _(dve):
                for s in range(2):
                    nc.vector.memset(u[s][:, :, R:R + W], 0.0)
                    nc.vector.memset(u[s][:, :, 0:R], NEG)
                    nc.vector.memset(u[s][:, :, R + W:UC], NEG)
                nc.vector.memset(x1[1][:], 0.0).then_inc(pads_set, 1)
                dve.sem_inc(a_done, NA)
                dve.sem_inc(b_done, NB)
                dve.sem_inc(joined, 1)
                dve.sem_inc(chunk_done, CPW)
                with nc.Fori(0, NWIN // 2, engines=DVE_ONLY) as i:
                    for s in range(2):
                        n = i * 2 + s
                        for k in range(CPW):
                            c = i * CH_IT + (s * CPW + k)
                            a_count = 0
                            for kind, j in order:
                                if kind == "pe":
                                    if j == 0:
                                        dve.wait_ge(b_started, c + 1)
                                    dve.wait_ge(m_pe_ready, at(c, NB, j + 1))
                                    dve.wait_ge(b_done, at(c, NB, j - 1))
                                    di, base, outer = pe_pairs[j // 2]
                                    part = acc_b[:, (j % 2) * (CR // 2):(j % 2 + 1) * (CR // 2), :]
                                    nc.vector.scalar_tensor_tensor(
                                        out=part, in0=m_pe[j % 2][:], scalar=kt[:, col(di, base):col(di, base) + 1],
                                        in1=part, op0=ALU.subtract, op1=ALU.max).then_inc(b_done, 1)
                                    continue
                                if a_count == 0:
                                    dve.wait_ge(a_started, c + 1)
                                if kind == "pool":
                                    dve.wait_ge(m_pool_ready, at(c, NPOOL, j + 1))
                                    di, base, outer = pool_pairs[j]
                                    src = m_pool[j % 2][:]
                                else:
                                    di, base = rest[j]
                                    src = u[s][:, k * CR + di:k * CR + di + CR, base:base + W]
                                dve.wait_ge(a_done, at(c, NA, a_count))
                                nc.vector.scalar_tensor_tensor(
                                    out=acc_a[:], in0=src, scalar=kt[:, col(di, base):col(di, base) + 1],
                                    in1=acc_a[:], op0=ALU.subtract, op1=ALU.max).then_inc(a_done, 1)
                                a_count += 1
                            dve.wait_ge(a_done, at(c, NA, NA))
                            dve.wait_ge(b_done, at(c, NB, NB))
                            nc.vector.tensor_tensor(acc_a[:], acc_a[:], acc_b[:], ALU.max).then_inc(joined, 1)
                            dve.wait_ge(joined, at(c, 1, 1))
                            dve.wait_ge(xc_loaded[k], n * 16 + 16)
                            dve.wait_ge(x1_summed, c * 2 + 2)
                            dve.wait_ge(x1_stored[k], n * 16 + 16)
                            nc.vector.tensor_tensor(x1[k][:], acc_a[:], xc[k][:], ALU.add).then_inc(chunk_done, 1)


def convolution(nc, x1_pl, h_pl, proj_w, mats, par, shift1, sums1, eps, conv_in, h_shift, h_sums):
    HR = WR + 2
    QR = 4
    PARTS = WR // QR
    rows_of = [(0, 1)] + [(1 + q * QR, 1 + (q + 1) * QR) for q in range(PARTS)] + [(HR - 1, HR)]
    NPROJ = len(rows_of)
    with ExitStack() as ctx:
        def sb(name, shape):
            return ctx.enter_context(nc.sbuf_tensor(name, shape, F32))

        def sem(name):
            return ctx.enter_context(nc.semaphore(name))

        xs = [sb(f"xs{s}", [P, HR, W]) for s in range(2)]
        o = [sb(f"o{s}", [P, HR, W + 2]) for s in range(2)]
        h = [sb(f"h{s}", [P, WR, W]) for s in range(2)]
        waste = sb("waste", [P, WR, W])
        ybar = sb("ybar", [P, 2, GROUPS])
        obar = sb("obar", [P, GROUPS])
        wsum = sb("wsum", [P, 1])
        wbd = sb("wbd", [P, P])
        wt = sb("wt", [P, P])
        wg = sb("wg", [P, GROUPS, P])
        diag = sb("diag", [P, TAPS_PE, P])
        evac = sb("evac", [P, 2, 3, NWIN])
        mom = sb("mom", [P, 2, GROUPS])
        gm = sb("gm2", [P, 2, GROUPS])
        var = sb("var2", [P, GROUPS])
        std = sb("std2", [P, GROUPS])
        cb = sb("cb", [P, GROUPS])
        pp = [ctx.enter_context(nc.psum_tensor(f"pp{s}", [P, QR, W], F32)) for s in range(2)]
        hp = [ctx.enter_context(nc.psum_tensor(f"hp{s}", [P, QR, W], F32)) for s in range(2)]

        blocks_zero = sem("blocks_zero")
        proj_loaded = sem("proj_loaded")
        step = sem("step2")
        sums_ready = sem("sums_ready")
        means_ready = sem("means_ready2")
        var_ready = sem("var_ready2")
        std_ready = sem("std_ready2")
        bias_ready = sem("bias_ready")
        wt_ready = sem("wt_ready")
        pt_ready = sem("pt_ready")
        tables_ready = sem("tables_ready")
        xs_loaded = [sem(f"xs_loaded{s}") for s in range(2)]
        projected = sem("projected")
        evacuated = sem("evacuated")
        taps_ready = sem("taps_ready")
        taps_used = sem("taps_used")
        h_chain = sem("h_chain")
        h_stored = [sem(f"h_stored{s}") for s in range(2)]
        act_turns, sp_turns = sem("act_turns2"), sem("sp_turns2")
        h_summed = sem("h_summed")
        obar_ready = sem("obar_ready")
        hbar_ready = sem("hbar_ready")
        CHAIN = 9 - TAPS_PE - 1

        with nc.Block() as block:
            @block.sync
            def _(sp):
                def load(w, g, slot, top=False, bottom=False):
                    lo, n = (1, HR - 1) if top else (0, HR - 1 if bottom else HR)
                    first = w * (WR * W) + (0 if top else -W)
                    sp.dma_start(xs[slot][:, lo:lo + n, :],
                                 x1_pl[g * P:(g + 1) * P, bass.ds(first, n * W)]
                                 .rearrange("p (r w) -> p r w", w=W)).then_inc(xs_loaded[slot], 16)

                def window(n, w, slot, g, ahead_w, ahead_g, top=False, bottom=False):
                    sp.wait_ge(projected, n * NPROJ + NPROJ)
                    passed(sp, sp_turns)
                    if ahead_w is not None:
                        load(ahead_w, ahead_g, slot, top, bottom)
                    sp.wait_ge(h_chain, n * (2 * CHAIN) + (4 * CHAIN + 1))
                    passed(sp, sp_turns)
                    sp.dma_start(h_pl[g * P:(g + 1) * P, bass.ds(w * (WR * W), WR * W)],
                                 h[slot][:].rearrange("p r w -> p (r w)")).then_inc(h_stored[slot], 16)

                sp.wait_ge(blocks_zero, 1)
                for b in range(IMG):
                    sp.dma_start(wbd[b * CH:(b + 1) * CH, b * CH:(b + 1) * CH], proj_w).then_inc(proj_loaded, 16)
                sp.sem_inc(h_stored[0], 16)
                sp.sem_inc(h_stored[1], 16)
                load(0, 0, 0, top=True)
                load(1, 0, 1)
                for g in range(GROUPS):
                    base = g * WIN
                    with nc.Fori(0, (WIN - 4) // 2, engines=SP_ONLY) as i:
                        for s in range(2):
                            w = i * 2 + s
                            window(w + base, w, s, g, w + 2, g)
                    ahead = g + 1 < GROUPS
                    window(base + WIN - 4, WIN - 4, 0, g, WIN - 2, g)
                    window(base + WIN - 3, WIN - 3, 1, g, WIN - 1, g, bottom=True)
                    window(base + WIN - 2, WIN - 2, 0, g, 0 if ahead else None, g + 1, top=True)
                    window(base + WIN - 1, WIN - 1, 1, g, 1 if ahead else None, g + 1)
                for s in range(2):
                    sp.wait_ge(h_stored[s], (NWIN // 2 + 1) * 16)

            @block.tensor
            def _(pe):
                pe.wait_ge(sums_ready, 1)
                nc.tensor.matmul(hp[0][:, 0, 0:4], mats[:, 1, :], mom[:].rearrange("p t g -> p (t g)"),
                                 start=True, stop=True).then_inc(means_ready, 1)
                pe.wait_ge(proj_loaded, IMG * 16)
                nc.tensor.matmul(pp[0][:, 0, 0:P], wbd[:], mats[:, 0, :], start=True, stop=True) \
                    .then_inc(pt_ready, 1)
                pe.wait_ge(wt_ready, 1)
                pe.wait_ge(bias_ready, 1)
                nc.tensor.matmul(pp[1][:, 0, 0:2 * GROUPS], wt[:], ybar[:].rearrange("p t g -> p (t g)"),
                                 start=True, stop=True).then_inc(pt_ready, 1)
                pe.wait_ge(obar_ready, 1)
                nc.tensor.matmul(hp[1][:, 0, 0:GROUPS], mats[:, 2, :], obar[:], start=True, stop=True) \
                    .then_inc(hbar_ready, 1)
                pe.wait_ge(tables_ready, 1)

                def project(n, s, g, e):
                    lo, hi = rows_of[e]
                    pe.wait_ge(evacuated, n * NPROJ + (NPROJ + e - 1))
                    for r in range(lo, hi, 2):
                        top = min(r + 2, hi)
                        last = nc.tensor.matmul(pp[e % 2][:, r - lo:top - lo, :], wg[:, g, :], xs[s][:, r:top, :],
                                                start=True, stop=True)
                    last.then_inc(projected, 1)

                def taps(n, s, q):
                    pe.wait_ge(evacuated, n * NPROJ + (NPROJ + q + 3))
                    pe.wait_ge(taps_used, n * PARTS + (PARTS + q - 1))
                    for r in range(0, QR, 2):
                        for t in range(TAPS_PE):
                            ty, tx = divmod(t, 3)
                            top = q * QR + r + ty
                            last = nc.tensor.matmul(hp[q % 2][:, r:r + 2, :], diag[:, t, :],
                                                    o[s][:, top:top + 2, tx:tx + W],
                                                    start=(t == 0), stop=(t == TAPS_PE - 1))
                    last.then_inc(taps_ready, 1)

                for g in range(GROUPS):
                    with nc.Fori(0, WIN // 2, engines=PE_ONLY) as i:
                        for s in range(2):
                            n = i * 2 + (g * WIN + s)
                            pe.wait_ge(xs_loaded[s], i * 16 + (g * WIN // 2 + 1) * 16)
                            for e in range(4):
                                project(n, s, g, e)
                            for q in range(PARTS):
                                taps(n, s, q)
                                if 4 + q < NPROJ:
                                    project(n, s, g, 4 + q)

            @block.scalar
            def _(act):
                act.wait_ge(var_ready, 1)
                nc.scalar.activation(std[:], var[:], ACT.Sqrt, bias=eps[:, 0:1]).then_inc(std_ready, 1)
                act.sem_inc(evacuated, NPROJ)
                act.sem_inc(h_summed, 1)
                act.wait_ge(tables_ready, 1)

                def sums_before(n, s):
                    act.wait_ge(h_chain, n * (2 * CHAIN) + (2 * CHAIN + 1))
                    act.wait_ge(h_summed, n * 2 + 1)
                    passed(act, act_turns)
                    nc.scalar.activation(waste[:], h[1 - s][:], ACT.Identity, bias=h_shift[:, 0:1],
                                         accum_out=h_sums[:, 0, bass.ds(n, 1)]).then_inc(h_summed, 1)
                    act.wait_ge(h_summed, n * 2 + 2)
                    passed(act, act_turns)
                    nc.scalar.activation(waste[:], h[1 - s][:], ACT.Square, bias=h_shift[:, 0:1],
                                         accum_out=h_sums[:, 1, bass.ds(n, 1)]).then_inc(h_summed, 1)

                with nc.Fori(0, NWIN // 2, engines=ACT_ONLY) as i:
                    for s in range(2):
                        n = i * 2 + s
                        for e, (lo, hi) in enumerate(rows_of):
                            if e == 0:
                                act.wait_ge(h_chain, n * (2 * CHAIN) + 1)
                            kind = 0 if e == 0 else 2 if e == NPROJ - 1 else 1
                            act.wait_ge(projected, n * NPROJ + (e + 1))
                            passed(act, act_turns)
                            nc.scalar.activation(o[s][:, lo:hi, 1:W + 1], pp[e % 2][:, 0:hi - lo, :], ACT.Identity,
                                                 bias=evac[:, 1, kind, bass.ds(n, 1)],
                                                 scale=evac[:, 0, kind, bass.ds(n, 1)]).then_inc(evacuated, 1)
                        sums_before(n, s)
                sums_before(NWIN, 0)

            @block.vector
            def _(dve):
                steps = [0]

                def link(ins):
                    steps[0] += 1
                    ins.then_inc(step, 1)
                    dve.wait_ge(step, steps[0])

                nc.vector.memset(wbd[:], 0.0)
                for s in range(2):
                    nc.vector.memset(o[s][:], 0.0)
                    nc.vector.memset(h[s][:], 0.0)
                    last = nc.vector.memset(xs[s][:], 0.0)
                last.then_inc(blocks_zero, 1)
                view = sums1[:, :, 1:].rearrange("p t (g c) -> p t g c", g=GROUPS)
                for t in range(2):
                    link(nc.vector.tensor_reduce(mom[:, t, :], view[:, t, :, :], mybir.AxisListType.X, ALU.add))
                nc.vector.tensor_scalar(mom[:], mom[:], 1.0 / (H * W), None, ALU.mult).then_inc(sums_ready, 1)
                dve.wait_ge(means_ready, 1)
                link(nc.vector.tensor_copy(gm[:].rearrange("p t g -> p (t g)"), hp[0][:, 0, 0:4]))
                link(nc.vector.tensor_tensor(var[:], gm[:, 0, :], gm[:, 0, :], ALU.mult))
                nc.vector.tensor_tensor(var[:], gm[:, 1, :], var[:], ALU.subtract).then_inc(var_ready, 1)
                dve.wait_ge(std_ready, 1)
                link(nc.vector.reciprocal(conv_in[:, :, 0], std[:]))
                link(nc.vector.tensor_tensor(ybar[:, 0, :], mom[:, 0, :], gm[:, 0, :], ALU.subtract))
                link(nc.vector.tensor_tensor(ybar[:, 0, :], ybar[:, 0, :], conv_in[:, :, 0], ALU.mult))
                link(nc.vector.tensor_tensor(gm[:, 0, :], gm[:, 0, :], shift1[:, 1:NWIN + 1:WIN], ALU.subtract))
                link(nc.vector.scalar_tensor_tensor(out=conv_in[:, :, 1], in0=gm[:, 0, :], scalar=-1.0,
                                                    in1=conv_in[:, :, 0], op0=ALU.mult, op1=ALU.mult))
                nc.vector.tensor_copy(ybar[:, 1, :], conv_in[:, :, 1]).then_inc(bias_ready, 1)
                dve.wait_ge(pt_ready, 1)
                nc.vector.tensor_copy(wt[:], pp[0][:, 0, 0:P]).then_inc(wt_ready, 1)
                for g in range(GROUPS):
                    link(nc.vector.tensor_scalar(wg[:, g, :], pp[0][:, 0, 0:P], conv_in[:, g, 0:1], None, ALU.mult))
                for t in range(TAPS_PE):
                    link(nc.vector.tensor_scalar(diag[:, t, :], mats[:, 0, :], par[:, COL_DW + t:COL_DW + t + 1],
                                                 None, ALU.mult))
                dve.wait_ge(pt_ready, 2)
                link(nc.vector.tensor_scalar(cb[:], pp[1][:, 0, GROUPS:2 * GROUPS], par[:, COL_PB:COL_PB + 1],
                                             None, ALU.add))
                nc.vector.tensor_scalar(obar[:], pp[1][:, 0, 0:GROUPS], par[:, COL_PB:COL_PB + 1], None,
                                        ALU.add).then_inc(obar_ready, 1)
                link(nc.vector.tensor_reduce(wsum[:], par[:, COL_DW:COL_DW + 9], mybir.AxisListType.X, ALU.add))
                dve.wait_ge(hbar_ready, 1)
                link(nc.vector.tensor_reduce(h_shift[:], hp[1][:, 0, 0:GROUPS], mybir.AxisListType.X, ALU.add))
                link(nc.vector.tensor_scalar(h_shift[:], h_shift[:], wsum[:, 0:1], -1.0 / GROUPS, ALU.mult, ALU.mult))
                link(nc.vector.memset(evac[:], 1.0))
                for g in range(GROUPS):
                    lo, hi = g * WIN, (g + 1) * WIN
                    link(nc.vector.tensor_scalar(evac[:, 1, :, lo:hi], evac[:, 1, :, lo:hi], cb[:, g:g + 1], None,
                                                 ALU.mult))
                    for kind, w in ((0, lo), (2, hi - 1)):
                        link(nc.vector.memset(evac[:, :, kind, w:w + 1], 0.0))
                nc.vector.memset(cb[:], 0.0).then_inc(tables_ready, 1)
                dve.sem_inc(taps_used, PARTS)
                dve.sem_inc(h_chain, 2 * CHAIN + 1)
                with nc.Fori(0, NWIN // 2, engines=DVE_ONLY) as i:
                    for s in range(2):
                        n = i * 2 + s
                        dve.wait_ge(h_stored[s], i * 16 + 16)
                        dve.wait_ge(h_summed, n * 2 + 1)
                        for half in range(2):
                            for q in range(half * PARTS // 2, (half + 1) * PARTS // 2):
                                dve.wait_ge(taps_ready, n * PARTS + (q + 1))
                                ty, tx = divmod(TAPS_PE, 3)
                                nc.vector.scalar_tensor_tensor(
                                    out=h[s][:, q * QR:(q + 1) * QR, :],
                                    in0=o[s][:, q * QR + ty:(q + 1) * QR + ty, tx:tx + W],
                                    scalar=par[:, COL_DW + TAPS_PE:COL_DW + TAPS_PE + 1],
                                    in1=hp[q % 2][:], op0=ALU.mult, op1=ALU.add).then_inc(taps_used, 1)
                            dve.wait_ge(taps_used, n * PARTS + (PARTS + (half + 1) * PARTS // 2))
                            lo = half * WR // 2
                            for t in range(TAPS_PE + 1, 9):
                                ty, tx = divmod(t, 3)
                                last = nc.vector.scalar_tensor_tensor(
                                    out=h[s][:, lo:lo + WR // 2, :],
                                    in0=o[s][:, lo + ty:lo + ty + WR // 2, tx:tx + W],
                                    scalar=par[:, COL_DW + t:COL_DW + t + 1],
                                    in1=h[s][:, lo:lo + WR // 2, :], op0=ALU.mult, op1=ALU.add) \
                                    .then_inc(h_chain, 1)
                                dve.wait_ge(h_chain, n * (2 * CHAIN) + ((2 + half) * CHAIN + 1 + t - TAPS_PE))


def resample(nc, x1_pl, h_pl, out_pl, mats, par, eps, conv_in, h_shift, h_sums):
    VR = 8
    NV = H // VR
    NALL = GROUPS * NV
    PR = 4
    with ExitStack() as ctx:
        def sb(name, shape):
            return ctx.enter_context(nc.sbuf_tensor(name, shape, F32))

        def sem(name):
            return ctx.enter_context(nc.semaphore(name))

        hw = [sb(f"hw{s}", [P, VR, W]) for s in range(2)]
        xw = [sb(f"xw{s}", [P, VR + 1, W]) for s in range(2)]
        y = [sb(f"y{s}", [P, VR + 1, W + 1]) for s in range(2)]
        ge = [sb(f"ge{s}", [P, VR, W]) for s in range(2)]
        z = [sb(f"z{s}", [P, VR, W]) for s in range(2)]
        dv = [sb(f"dv{s}", [P, VR, W + 1]) for s in range(2)]
        dd = [sb(f"dd{s}", [P, VR, W]) for s in range(2)]
        dh = [sb(f"dh{s}", [P, VR, W]) for s in range(2)]
        f = sb("f", [P, PR, W])
        res = [sb(f"res{s}", [P, VR, W]) for s in range(2)]
        off = sb("off", [P, 2, P])
        tab = sb("tab", [P, 6, NALL + 2])
        mv = sb("mv3", [P, 2])
        cm = sb("cm3", [P, 2])
        bn = sb("bn3", [P, 4])
        tx = [ctx.enter_context(nc.psum_tensor(f"tx{s}", [P, PR, W], F32)) for s in range(2)]
        ty = ctx.enter_context(nc.psum_tensor("ty", [P, PR, W], F32))
        ph = ctx.enter_context(nc.psum_tensor("ph", [P, PR, W], F32))

        step = sem("step3")
        moments_ready = sem("moments_ready3")
        means_ready = sem("means_ready3")
        var_ready = sem("var_ready3")
        std_ready = sem("std_ready3")
        tables_ready = sem("tables_ready3")
        hw_loaded = [sem(f"hw_loaded{s}") for s in range(2)]
        xw_loaded = [sem(f"xw_loaded{s}") for s in range(2)]
        y_ready = sem("y_ready")
        z_ready = sem("z_ready")
        ge_ready = sem("ge_ready")
        off_x = sem("off_x")
        off_y = sem("off_y")
        tanh_x = sem("tanh_x")
        tanh_y = sem("tanh_y")
        diffs = sem("diffs")
        part_x = sem("part_x")
        part_y = sem("part_y")
        chain = sem("chain3")
        stored = [sem(f"stored{s}") for s in range(2)]
        act_turns, sp_turns = sem("act_turns3"), sem("sp_turns3")

        with nc.Block() as block:
            @block.sync
            def _(sp):
                def load(w, g, slot, bottom=False):
                    n = VR if bottom else VR + 1
                    sp.dma_start(xw[slot][:, 0:n, :].rearrange("p r w -> p (r w)"),
                                 x1_pl[g * P:(g + 1) * P, bass.ds(w * (VR * W), n * W)]) \
                        .then_inc(xw_loaded[slot], 16)
                    sp.dma_start(hw[slot][:].rearrange("p r w -> p (r w)"),
                                 h_pl[g * P:(g + 1) * P, bass.ds(w * (VR * W), VR * W)]) \
                        .then_inc(hw_loaded[slot], 16)

                def window(n, w, slot, g, ahead_w, ahead_g, bottom=False):
                    sp.wait_ge(z_ready, n + 1)
                    sp.wait_ge(ge_ready, n + 1)
                    passed(sp, sp_turns)
                    load(ahead_w, ahead_g, slot, bottom)
                    sp.wait_ge(part_y, n * 2 + 5)
                    passed(sp, sp_turns)
                    sp.dma_start(out_pl[g * P:(g + 1) * P, bass.ds(w * (VR * W), VR * W)],
                                 res[slot][:].rearrange("p r w -> p (r w)")).then_inc(stored[slot], 16)

                sp.wait_ge(tables_ready, 1)
                sp.sem_inc(stored[0], 16)
                sp.sem_inc(stored[1], 16)
                load(0, 0, 0)
                load(1, 0, 1)
                for g in range(GROUPS):
                    base = g * NV
                    with nc.Fori(0, (NV - 4) // 2, engines=SP_ONLY) as i:
                        for s in range(2):
                            w = i * 2 + s
                            window(w + base, w, s, g, w + 2, g)
                    ahead = min(g + 1, GROUPS - 1)
                    window(base + NV - 4, NV - 4, 0, g, NV - 2, g)
                    window(base + NV - 3, NV - 3, 1, g, NV - 1, g, bottom=True)
                    window(base + NV - 2, NV - 2, 0, g, 0, ahead)
                    window(base + NV - 1, NV - 1, 1, g, 1, ahead)
                for s in range(2):
                    sp.wait_ge(xw_loaded[s], (NALL // 2 + 1) * 16)
                    sp.wait_ge(hw_loaded[s], (NALL // 2 + 1) * 16)
                    sp.wait_ge(stored[s], (NALL // 2 + 1) * 16)

            @block.tensor
            def _(pe):
                pe.wait_ge(moments_ready, 1)
                nc.tensor.matmul(ph[:, 0, 0:2], mats[:, 2, :], mv[:], start=True, stop=True).then_inc(means_ready, 1)
                pe.wait_ge(tables_ready, 1)
                with nc.Fori(0, NALL // 2, engines=PE_ONLY) as i:
                    for s in range(2):
                        n = i * 2 + s
                        pe.wait_ge(ge_ready, n + 1)
                        for p in range(2):
                            pe.wait_ge(part_x, n * 2 + (p + 1))
                            for r in range(0, PR, 2):
                                last = nc.tensor.matmul(tx[p][:, r:r + 2, :], off[:, 1, :],
                                                        ge[s][:, p * PR + r:p * PR + r + 2, :],
                                                        start=True, stop=True)
                            last.then_inc(off_x, 1)
                            pe.wait_ge(part_y, n * 2 + (p + 3))
                            for r in range(0, PR, 2):
                                last = nc.tensor.matmul(ty[:, r:r + 2, :], off[:, 0, :],
                                                        ge[s][:, p * PR + r:p * PR + r + 2, :],
                                                        start=True, stop=True)
                            last.then_inc(off_y, 1)

            @block.scalar
            def _(act):
                def make_y(n, s, loads):
                    act.wait_ge(xw_loaded[s], loads * 16)
                    act.wait_ge(diffs, n * 3 + 3)
                    passed(act, act_turns)
                    for k, (lo, hi) in enumerate(((0, VR), (VR, VR + 1))):
                        nc.scalar.activation(y[s][:, lo:hi, 0:W], xw[s][:, lo:hi, :], ACT.Identity,
                                             bias=tab[:, 2 * k + 1, bass.ds(n, 1)],
                                             scale=tab[:, 2 * k, bass.ds(n, 1)]).then_inc(y_ready, 1)

                def make_ge(n, s, loads):
                    act.wait_ge(hw_loaded[s], loads * 16)
                    act.wait_ge(off_y, n * 2 + 2)
                    nc.scalar.activation(ge[s][:], hw[s][:], ACT.Gelu, bias=bn[:, 3:4], scale=bn[:, 2:3]) \
                        .then_inc(ge_ready, 1)

                def make_z(n, s):
                    act.wait_ge(part_y, n * 2 + 1)
                    passed(act, act_turns)
                    nc.scalar.activation(z[s][:], xw[s][:, 0:VR, :], ACT.Identity,
                                         bias=tab[:, 5, bass.ds(n, 1)],
                                         scale=tab[:, 4, bass.ds(n, 1)]).then_inc(z_ready, 1)

                def make_tanh_x(n, p):
                    act.wait_ge(off_x, n * 2 + (p + 1))
                    nc.scalar.activation(tx[p][:], tx[p][:], ACT.Tanh).then_inc(tanh_x, 1)

                def make_tanh_y(n, p):
                    act.wait_ge(off_y, n * 2 + (p + 1 + 4))
                    nc.scalar.activation(ty[:], ty[:], ACT.Tanh).then_inc(tanh_y, 1)

                act.wait_ge(var_ready, 1)
                nc.scalar.activation(bn[:, 1:2], bn[:, 0:1], ACT.Sqrt, bias=eps[:, 0:1]).then_inc(std_ready, 1)
                act.wait_ge(tables_ready, 1)
                make_y(0, 0, 1)
                make_y(1, 1, 1)
                make_ge(0, 0, 1)
                make_z(0, 0)
                with nc.Fori(0, NALL // 2, engines=ACT_ONLY) as i:
                    for s in range(2):
                        n = i * 2 + s
                        make_tanh_x(n, 0)
                        make_tanh_y(n, 0)
                        make_tanh_x(n, 1)
                        make_z(n + 1, 1 - s)
                        make_ge(n + 1, 1 - s, i + (1 + s))
                        make_tanh_y(n, 1)
                        make_y(n + 2, s, i + 2)

            @block.gpsimd
            def _(pool):
                pool.sem_inc(diffs, 6)
                with nc.Fori(0, NALL // 2, engines=POOL_ONLY) as i:
                    for s in range(2):
                        n = i * 2 + s
                        pool.wait_ge(y_ready, n * 2 + 2)
                        pool.wait_ge(part_y, n * 2 + 1)
                        nc.gpsimd.tensor_tensor(dh[s][:], y[s][:, 0:VR, 1:W + 1], y[s][:, 0:VR, 0:W],
                                                ALU.subtract).then_inc(diffs, 1)
                        nc.gpsimd.tensor_tensor(dv[s][:], y[s][:, 1:VR + 1, :], y[s][:, 0:VR, :],
                                                ALU.subtract).then_inc(diffs, 1)
                        pool.wait_ge(diffs, n * 3 + 8)
                        nc.gpsimd.tensor_tensor(dd[s][:], dv[s][:, :, 1:W + 1], dv[s][:, :, 0:W],
                                                ALU.subtract).then_inc(diffs, 1)

            @block.vector
            def _(dve):
                steps = [0]

                def link(ins):
                    steps[0] += 1
                    ins.then_inc(step, 1)
                    dve.wait_ge(step, steps[0])

                for s in range(2):
                    nc.vector.memset(y[s][:], 0.0)
                    nc.vector.memset(xw[s][:], 0.0)
                link(nc.vector.memset(tab[:], 1.0))
                for t in range(2):
                    link(nc.vector.tensor_reduce(mv[:, t:t + 1], h_sums[:, t, 1:], mybir.AxisListType.X, ALU.add))
                nc.vector.tensor_scalar(mv[:], mv[:], 1.0 / (GROUPS * H * W), None, ALU.mult) \
                    .then_inc(moments_ready, 1)
                dve.wait_ge(means_ready, 1)
                link(nc.vector.tensor_copy(cm[:], ph[:, 0, 0:2]))
                link(nc.vector.tensor_tensor(bn[:, 0:1], cm[:, 0:1], cm[:, 0:1], ALU.mult))
                nc.vector.tensor_tensor(bn[:, 0:1], cm[:, 1:2], bn[:, 0:1], ALU.subtract).then_inc(var_ready, 1)
                dve.wait_ge(std_ready, 1)
                link(nc.vector.reciprocal(bn[:, 2:3], bn[:, 1:2]))
                link(nc.vector.tensor_tensor(bn[:, 2:3], bn[:, 2:3], par[:, COL_BG:COL_BG + 1], ALU.mult))
                link(nc.vector.tensor_tensor(cm[:, 0:1], cm[:, 0:1], h_shift[:], ALU.subtract))
                link(nc.vector.tensor_tensor(cm[:, 0:1], cm[:, 0:1], par[:, COL_DB:COL_DB + 1], ALU.add))
                link(nc.vector.tensor_tensor(cm[:, 0:1], par[:, COL_DB:COL_DB + 1], cm[:, 0:1], ALU.subtract))
                link(nc.vector.scalar_tensor_tensor(out=bn[:, 3:4], in0=cm[:, 0:1], scalar=bn[:, 2:3],
                                                    in1=par[:, COL_BB:COL_BB + 1], op0=ALU.mult, op1=ALU.add))
                for t in range(2):
                    link(nc.vector.tensor_scalar(off[:, t, :], mats[:, 3, :],
                                                 par[:, COL_OFF + t:COL_OFF + t + 1], None, ALU.mult))
                for g in range(GROUPS):
                    lo, hi = g * NV, (g + 1) * NV + 2 * (g == GROUPS - 1)
                    for t in range(2):
                        for row in (t, 2 + t):
                            link(nc.vector.tensor_scalar(tab[:, row, lo:hi], tab[:, row, lo:hi],
                                                         conv_in[:, g, t:t + 1], 0.5, ALU.mult, ALU.mult))
                    link(nc.vector.tensor_scalar(tab[:, 4, lo:hi], tab[:, 4, lo:hi],
                                                 conv_in[:, g, 0:1], None, ALU.add))
                    link(nc.vector.tensor_scalar(tab[:, 5, lo:hi], tab[:, 5, lo:hi],
                                                 conv_in[:, g, 1:2], None, ALU.mult))
                    link(nc.vector.memset(tab[:, 2:4, lo + NV - 1:lo + NV], 0.0))
                dve.sem_inc(part_x, 2)
                dve.sem_inc(part_y, 3)
                dve.sem_inc(off_y, 4)
                nc.vector.memset(cm[:], 0.0).then_inc(tables_ready, 1)
                with nc.Fori(0, NALL // 2, engines=DVE_ONLY) as i:
                    for s in range(2):
                        n = i * 2 + s
                        for p in range(2):
                            at = n * 8 + 4 * p
                            rows = slice(p * PR, (p + 1) * PR)
                            part = n * 2 + (p + 1)
                            if p == 0:
                                dve.wait_ge(stored[s], i * 16 + 16)
                                dve.wait_ge(z_ready, n + 1)
                                dve.wait_ge(diffs, n * 3 + 9)
                            dve.wait_ge(tanh_x, part)
                            nc.vector.scalar_tensor_tensor(out=ph[:], in0=tx[p][:], scalar=1.0, in1=dh[s][:, rows, :],
                                                           op0=ALU.add, op1=ALU.mult).then_inc(chain, 1)
                            nc.vector.scalar_tensor_tensor(out=tx[p][:], in0=tx[p][:], scalar=1.0,
                                                           in1=dd[s][:, rows, :],
                                                           op0=ALU.add, op1=ALU.mult).then_inc(chain, 1)
                            dve.wait_ge(chain, at + 1)
                            nc.vector.tensor_tensor(res[s][:, rows, :], ph[:], z[s][:, rows, :], ALU.add) \
                                .then_inc(chain, 1)
                            dve.wait_ge(chain, at + 2)
                            nc.vector.scalar_tensor_tensor(out=f[:], in0=tx[p][:], scalar=0.5,
                                                           in1=dv[s][:, rows, 0:W],
                                                           op0=ALU.mult, op1=ALU.add).then_inc(part_x, 1)
                            dve.wait_ge(part_x, part + 2)
                            dve.wait_ge(tanh_y, part)
                            nc.vector.scalar_tensor_tensor(out=ty[:], in0=ty[:], scalar=1.0, in1=f[:],
                                                           op0=ALU.add, op1=ALU.mult).then_inc(chain, 1)
                            dve.wait_ge(chain, at + 4)
                            nc.vector.tensor_tensor(res[s][:, rows, :], ty[:], res[s][:, rows, :], ALU.add) \
                                .then_inc(part_y, 1)


def kernel(**inputs):
    import concourse.bacc as bacc
    from concourse.bass_utils import run_bass_kernel_spmd

    a = {k: np.asarray(v) for k, v in inputs.items()}
    columns = [a["L0_conv_finsler_params"], a["L1_conv_proj_b"], a["L1_conv_dw_w"], a["L1_conv_dw_b"],
               a["L1_conv_bn_g"], a["L1_conv_bn_b"], a["L1_conv_off_w"].reshape(2, CH).T]
    params = np.concatenate([c.reshape(CH, -1) for c in columns], axis=1)
    basis, mats = shape_constants()
    arrays = {
        "x_dram": np.ascontiguousarray(a["x"]),
        "params_dram": np.ascontiguousarray(np.tile(params, (IMG, 1))),
        "proj_w_dram": np.ascontiguousarray(a["L1_conv_proj_w"].reshape(CH, CH)),
        "basis_dram": basis,
        "mats_dram": mats,
    }
    nc = bacc.Bacc("TRN2", target_bir_lowering=False, num_devices=1)
    args = [nc.dram_tensor(k, v.shape, F32, kind="ExternalInput").ap() for k, v in arrays.items()]
    out = nc.dram_tensor("out_dram", a["x"].shape, F32, kind="ExternalOutput").ap()
    build(nc, *args, out)
    r = run_bass_kernel_spmd(nc, [arrays], core_ids=[0])
    return r.results[0]["out_dram"]
```

```python
from contextlib import ExitStack

import concourse.bass as bass
import numpy as np
from concourse import mybir

F32 = mybir.dt.float32
ALU = mybir.AluOpType
ACT = mybir.ActivationFunctionType
DVE_ONLY = [mybir.EngineType.DVE]
ACT_ONLY = [mybir.EngineType.Activation]
PE_ONLY = [mybir.EngineType.PE]
POOL_ONLY = [mybir.EngineType.Pool]
SP_ONLY = [mybir.EngineType.SP]

P = 128
CH = 32
IMG = P // CH
H = W = 256
GROUPS = 8 // IMG
R = 5
KS = 2 * R + 1
WR = 16
WIN = H // WR
NWIN = GROUPS * WIN
UR, UC = WR + 2 * R, W + 2 * R
CR = 8
CPW = WR // CR
NEG = -1e30
EPS = 1e-5
ALPHA = 0.65
EXPO = 2.0 * ALPHA / (2.0 * ALPHA - 1.0)
NU = (2.0 * ALPHA - 1.0) * (2.0 * ALPHA) ** (-EXPO)
BANK = 512
FIRST_TRIPLE, PRE_TURNS, DMA_TURNS = 9, 7, 4
POOL_AT, PE_AT = 1.0, 1.1
TAPS_PE, TAPS_ACT = 2, 2

COL_FP, COL_PB, COL_DW, COL_DB, COL_BG, COL_BB, COL_OFF, COL_END = 0, 6, 7, 16, 17, 18, 19, 21


def passed(engine, turns):
    engine.sem_inc(turns, 1)


def dilation_plan(npool, npe, ntriples):
    triples = [(di, 8, 9, 10) for di in range(ntriples)]
    pairs = [(di, base, outer, None) for base, outer in ((5, 4), (3, 2), (6, 7), (1, 0)) for di in range(KS)]
    pairs += [(di, 8, 9, None) for di in range(ntriples, KS)]
    singles = [(di, 10) for di in range(ntriples, KS)]
    while ntriples + len(pairs) > npool + npe:
        di, base, outer, _ = pairs.pop()
        singles += [(di, base), (di, outer)]

    relus = [((j + 0.5) / npool, "pool", j) for j in range(npool)]
    relus += [((j + 0.3) / npe, "pe", j) for j in range(npe)]
    relus = [(kind, j) for _, kind, j in sorted(relus)]
    head = [("pe", 0), ("pool", 0), ("pool", 1), ("pe", 1)]
    relus = head + [x for x in relus if x not in head]
    first, last = FIRST_TRIPLE, len(relus) - 1
    where = [first + (last - first) * i // (ntriples - 1) for i in range(ntriples)]
    units = {"pool": [None] * npool, "pe": [None] * npe}
    rest = iter(pairs)
    for turn, (kind, j) in enumerate(relus):
        units[kind][j] = triples[where.index(turn)] if turn in where else next(rest)

    act, gpsimd = [], [("add", j) for j in range(npool)]
    for turn, (kind, j) in enumerate(relus):
        for i, w in enumerate(where):
            if turn == w - PRE_TURNS:
                act.append(("pre", i))
        act.append((kind, j))
    for i, w in enumerate(where):
        adds = sum(kind == "pool" for kind, _ in relus[:w - DMA_TURNS]) - 1
        gpsimd.insert(gpsimd.index(("add", adds)), ("dma", i))
    dve = [((j + POOL_AT) / npool, "pool", j) for j in range(npool)]
    dve += [((h + PE_AT) / (2 * npe), "pe", h) for h in range(2 * npe)]
    dve += [((j + 0.8) / (len(singles) - 1), "single", j) for j in range(len(singles) - 1)]
    dve = [(kind, j) for _, kind, j in sorted(dve)]
    dve = [("pool", 0)] + [x for x in dve if x != ("pool", 0)]
    return units["pool"], units["pe"], singles, act, gpsimd, dve


def shape_constants():
    coords = np.arange(-R, R + 1, dtype=np.float32)
    yy, xx = np.meshgrid(coords, coords, indexing="ij")
    rho = np.sqrt(xx * xx + yy * yy)
    theta = np.arctan2(yy, xx)
    basis = []
    for k in range(1, 7):
        m = (k + 1) // 2
        basis.append(np.cos(m * theta) if k % 2 == 1 else np.sin(m * theta))
    radial = (np.float32(NU) * rho ** np.float32(EXPO)).astype(np.float32)
    rows = np.stack(basis + [radial]).astype(np.float32).reshape(1, 7 * KS * KS)
    p = np.arange(P)
    ident = np.eye(P, dtype=np.float32)
    pair_mean = (p[:, None] // 2 == p[None, :] // 2).astype(np.float32) * np.float32(0.5)
    channel_mean = (p[:, None] % CH == p[None, :] % CH).astype(np.float32) * np.float32(1.0 / IMG)
    same_image = (p[:, None] // CH == p[None, :] // CH).astype(np.float32)
    return np.repeat(rows, P, 0), np.stack([ident, pair_mean, channel_mean, same_image], 1).copy()


def build(nc, x, params, proj_w, basis_in, mats_in, out):
    x_pl = x.rearrange("b c h w -> (b c) (h w)")
    out_pl = out.rearrange("b c h w -> (b c) (h w)")
    x1_pl = nc.dram_tensor("x1_scratch", (GROUPS * P, H * W), F32, kind="Internal").ap()
    h_pl = nc.dram_tensor("h_scratch", (GROUPS * P, H * W), F32, kind="Internal").ap()

    with ExitStack() as ctx:
        def sb(name, shape):
            return ctx.enter_context(nc.sbuf_tensor(name, shape, F32))

        mats = sb("mats", [P, 4, P])
        par = sb("par", [P, COL_END])
        kt = sb("kt", [P, KS * KS])
        nkt = sb("nkt", [P, KS * KS])
        gap_r = sb("gap_r", [P, KS * KS])
        gap_l = sb("gap_l", [P, KS * KS])
        norm1 = sb("norm1", [P, 2, 3, NWIN + 1])
        shift1 = sb("shift1", [P, NWIN + 1])
        sums1 = sb("sums1", [P, 2, NWIN * CPW + 1])
        eps = sb("eps", [P, 1])
        small = sb("small", [P, 64])
        ident = mats[:, 0, :]
        pair_mean = mats[:, 1, :]

        stats_and_tables(nc, x_pl, params, basis_in, mats_in, mats, par, kt, nkt, gap_r, gap_l,
                         norm1, shift1, eps, small, pair_mean)
        dilation(nc, x_pl, x1_pl, ident, kt, nkt, gap_r, gap_l, norm1, shift1, sums1)
        conv_in = sb("conv_in", [P, GROUPS, 2])
        h_shift = sb("h_shift", [P, 1])
        h_sums = sb("h_sums", [P, 2, NWIN + 1])
        convolution(nc, x1_pl, h_pl, proj_w, mats, par, shift1, sums1, eps, conv_in, h_shift, h_sums)
        resample(nc, x1_pl, h_pl, out_pl, mats, par, eps, conv_in, h_shift, h_sums)
    return nc


def stats_and_tables(nc, x_pl, params, basis_in, mats_in, mats, par, kt, nkt, gap_r, gap_l,
                     norm1, shift1, eps, small, pair_mean):
    TILE = 4096
    SLOTS = 4
    TILES = H * W // TILE
    SUB = TILE // BANK
    with ExitStack() as ctx:
        xt = ctx.enter_context(nc.sbuf_tensor("xt", [P, SLOTS, TILE], F32))
        stats = ctx.enter_context(nc.sbuf_tensor("stats", [P, GROUPS, TILES * SUB * 6], F32))
        bas = ctx.enter_context(nc.sbuf_tensor("bas", [P, 7, KS * KS], F32))
        ang = ctx.enter_context(nc.sbuf_tensor("ang", [P, KS * KS], F32))
        pstat = ctx.enter_context(nc.psum_tensor("pstat", [P, BANK], F32))
        consts_loaded = ctx.enter_context(nc.semaphore("consts_loaded"))
        tile_loaded = [ctx.enter_context(nc.semaphore(f"tile_loaded{s}")) for s in range(SLOTS)]
        tile_used = ctx.enter_context(nc.semaphore("tile_used"))
        sp_turns = ctx.enter_context(nc.semaphore("sp_turns1"))
        step = ctx.enter_context(nc.semaphore("step"))
        angle_ready = ctx.enter_context(nc.semaphore("angle_ready"))
        exp_ready = ctx.enter_context(nc.semaphore("exp_ready"))
        moments_ready = ctx.enter_context(nc.semaphore("moments_ready"))
        means_ready = ctx.enter_context(nc.semaphore("means_ready"))
        var_ready = ctx.enter_context(nc.semaphore("var_ready"))
        std_ready = ctx.enter_context(nc.semaphore("std_ready"))
        mv = small[:, 0:4].rearrange("p (g t) -> p g t", t=2)
        mom = small[:, 4:8].rearrange("p (g t) -> p g t", t=2)
        var = small[:, 8:10]
        rstd = small[:, 10:12]
        nbias = small[:, 12:14]
        gm = small[:, 14:18].rearrange("p (g t) -> p g t", t=2)

        with nc.Block() as block:
            @block.sync
            def _(sp):
                sp.dma_start(bas[:].rearrange("p k n -> p (k n)"), basis_in).then_inc(consts_loaded, 16)
                sp.dma_start(par[:], params).then_inc(consts_loaded, 16)
                sp.dma_start(mats[:], mats_in).then_inc(consts_loaded, 16)
                for g in range(GROUPS):
                    src = x_pl[g * P:(g + 1) * P, :]
                    for s in range(SLOTS):
                        t = g * TILES + s
                        if g > 0:
                            sp.wait_ge(tile_used, t - SLOTS + 1)
                        sp.dma_start(xt[:, s, :], src[:, s * TILE:(s + 1) * TILE]).then_inc(tile_loaded[s], 16)
                    with nc.Fori(1, TILES // SLOTS, engines=SP_ONLY) as i:
                        for s in range(SLOTS):
                            sp.wait_ge(tile_used, i * SLOTS + (g * TILES + s + 1 - SLOTS))
                            passed(sp, sp_turns)
                            sp.dma_start(xt[:, s, :], src[:, bass.ds(i * (SLOTS * TILE) + s * TILE, TILE)]) \
                                .then_inc(tile_loaded[s], 16)

            @block.vector
            def _(dve):
                steps = [0]

                def link(ins):
                    steps[0] += 1
                    ins.then_inc(step, 1)
                    dve.wait_ge(step, steps[0])

                link(nc.vector.memset(eps[:], EPS))
                dve.wait_ge(consts_loaded, 48)
                link(nc.vector.tensor_scalar(ang[:], bas[:, 0, :], par[:, COL_FP:COL_FP + 1], None, ALU.mult))
                for k in range(1, 6):
                    link(nc.vector.scalar_tensor_tensor(out=ang[:], in0=bas[:, k, :],
                                                        scalar=par[:, COL_FP + k:COL_FP + k + 1],
                                                        in1=ang[:], op0=ALU.mult, op1=ALU.add))
                nc.vector.sem_inc(angle_ready, 1)
                dve.wait_ge(exp_ready, 1)
                link(nc.vector.tensor_tensor(kt[:], ang[:], bas[:, 6, :], ALU.mult))
                link(nc.vector.tensor_scalar(nkt[:], kt[:], -1.0, None, ALU.mult))
                link(nc.vector.memset(gap_r[:], 0.0))
                link(nc.vector.memset(gap_l[:], 0.0))
                n = KS * KS
                link(nc.vector.tensor_tensor(gap_r[:, 0:n - 1], kt[:, 0:n - 1], kt[:, 1:n], ALU.subtract))
                link(nc.vector.tensor_tensor(gap_l[:, 1:n], kt[:, 1:n], kt[:, 0:n - 1], ALU.subtract))
                for g in range(GROUPS):
                    with nc.Fori(0, TILES // SLOTS, engines=DVE_ONLY) as i:
                        for s in range(SLOTS):
                            dve.wait_ge(tile_loaded[s], i * 16 + (g * (TILES // SLOTS) + 1) * 16)
                            for j in range(SUB):
                                at = i * (SLOTS * SUB * 6) + (s * SUB + j) * 6
                                last = nc.vector.bn_stats(stats[:, g, bass.ds(at, 6)],
                                                          xt[:, s, j * BANK:(j + 1) * BANK])
                            last.then_inc(tile_used, 1)
                dve.wait_ge(tile_used, GROUPS * TILES)
                for g in range(GROUPS):
                    link(nc.vector.bn_aggr(mv[:, g, :], stats[:, g, :]))
                link(nc.vector.tensor_tensor(mom[:, :, 1], mv[:, :, 0], mv[:, :, 0], ALU.mult))
                link(nc.vector.tensor_tensor(mom[:, :, 1], mom[:, :, 1], mv[:, :, 1], ALU.add))
                nc.vector.tensor_copy(mom[:, :, 0], mv[:, :, 0]).then_inc(moments_ready, 1)
                dve.wait_ge(means_ready, 1)
                link(nc.vector.tensor_copy(gm, pstat[:, 0:4].rearrange("p (g t) -> p g t", t=2)))
                link(nc.vector.tensor_tensor(var, gm[:, :, 0], gm[:, :, 0], ALU.mult))
                nc.vector.tensor_tensor(var, gm[:, :, 1], var, ALU.subtract).then_inc(var_ready, 1)
                dve.wait_ge(std_ready, 1)
                link(nc.vector.reciprocal(rstd, rstd))
                link(nc.vector.scalar_tensor_tensor(out=nbias, in0=gm[:, :, 0], scalar=-1.0, in1=rstd,
                                                    op0=ALU.mult, op1=ALU.mult))
                link(nc.vector.memset(norm1[:], 1.0))
                link(nc.vector.memset(shift1[:], 1.0))
                for g in range(GROUPS):
                    lo, hi = g * WIN, (g + 1) * WIN + (g == GROUPS - 1)
                    link(nc.vector.tensor_scalar(norm1[:, 0, :, lo:hi], norm1[:, 0, :, lo:hi],
                                                 rstd[:, g:g + 1], None, ALU.mult))
                    link(nc.vector.tensor_scalar(norm1[:, 1, :, lo:hi], norm1[:, 1, :, lo:hi],
                                                 nbias[:, g:g + 1], None, ALU.mult))
                    link(nc.vector.tensor_scalar(shift1[:, lo + 1:lo + WIN + 1], shift1[:, lo + 1:lo + WIN + 1],
                                                 gm[:, g, 0:1], -1.0, ALU.mult, ALU.mult))
                    for kind, w in ((0, lo), (2, lo + WIN - 1)):
                        link(nc.vector.memset(norm1[:, 0, kind, w:w + 1], 0.0))
                        link(nc.vector.memset(norm1[:, 1, kind, w:w + 1], NEG))

            @block.scalar
            def _(act):
                act.wait_ge(angle_ready, 1)
                act.wait_ge(step, 7)
                nc.scalar.activation(ang[:], ang[:], ACT.Exp, scale=-EXPO).then_inc(exp_ready, 1)
                act.wait_ge(var_ready, 1)
                nc.scalar.activation(rstd, var, ACT.Sqrt, bias=eps[:, 0:1]).then_inc(std_ready, 1)

            @block.tensor
            def _(pe):
                pe.wait_ge(moments_ready, 1)
                pe.wait_ge(consts_loaded, 48)
                nc.tensor.matmul(pstat[:, 0:4], pair_mean, small[:, 4:8], start=True, stop=True) \
                    .then_inc(means_ready, 1)


def dilation(nc, x_pl, x1_pl, ident, kt, nkt, gap_r, gap_l, norm1, shift1, sums1):
    NPOOL, NPE, NTRIPLE = 28, 20, 10
    NORM_PIECES = ((0, 0, R), (1, R, R + WR // 2), (1, R + WR // 2, R + WR), (2, R + WR, UR))
    NORM_TURNS = (15, 19, 23, 27)
    DX_PIECES = ((0, 5), (5, 9), (9, 13), (13, 17), (17, 21), (21, UR))
    DX_AT = ((0, 16), (0, 22), (0, 27), (1, 0), (1, 6), (1, 13))
    NU, ND = len(NORM_PIECES), len(DX_PIECES)
    START_TURN, SUMS_TURN = 4, 14
    pool_units, pe_units, singles, act_order, pool_order, dve_order = dilation_plan(NPOOL, NPE, NTRIPLE)
    init_b, *rest = singles
    NCHUNK = NWIN * CPW
    CH_IT = 2 * CPW

    NA = sum(kind != "pe" for kind, _ in dve_order)
    NB = 2 * NPE
    a_before = {}
    count = 0
    for kind, j in dve_order:
        count += kind != "pe"
        if kind == "pool":
            a_before[j] = count

    triple_no, triples, triple_relu = {}, [], []
    for kind, j in act_order:
        if kind != "pre":
            unit = (pool_units if kind == "pool" else pe_units)[j]
            if unit[3] is not None:
                triple_no[unit] = len(triples)
                triples.append(unit)
                triple_relu.append((kind, j))
    RUN = CR * UC - 2 * R

    def col(di, dj):
        return di * KS + dj

    with ExitStack() as ctx:
        def sb(name, shape):
            return ctx.enter_context(nc.sbuf_tensor(name, shape, F32))

        def sem(name):
            return ctx.enter_context(nc.semaphore(name))

        u = [sb(f"u{s}", [P, UR, UC]) for s in range(2)]
        dx = [sb(f"dx{s}", [P, UR, UC]) for s in range(2)]
        r_pool = [sb(f"r_pool{s}", [P, CR, W]) for s in range(2)]
        r_pe = [sb(f"r_pe{s}", [P, CR, W]) for s in range(2)]
        m_pool = [sb(f"m_pool{s}", [P, CR, W]) for s in range(2)]
        acc_b = sb("acc_b", [P, CR, W])
        xc = sb("xc", [P, CR, W])
        x1 = sb("x1", [P, CR, W])
        t = [sb(f"t{s}", [P, CR * UC]) for s in range(2)]
        acc_a = ctx.enter_context(nc.psum_tensor("acc_a", [P, CR, W], F32))
        m_pe = [ctx.enter_context(nc.psum_tensor(f"m_pe{s}", [P, CR // 2, W], F32)) for s in range(2)]

        pads_set = sem("pads_set")
        win_loaded = [sem(f"win_loaded{s}") for s in range(2)]
        xc_loaded = sem("xc_loaded")
        x1_stored = sem("x1_stored")
        x_added = sem("x_added")
        t_ready = sem("t_ready")
        t_added = [sem(f"t_added{s}") for s in range(2)]
        pool_turns = sem("pool_turns")
        u_ready = sem("u_ready")
        dx_ready = sem("dx_ready")
        r_pool_ready = sem("r_pool_ready")
        r_pe_ready = sem("r_pe_ready")
        m_pool_ready = sem("m_pool_ready")
        m_pe_ready = sem("m_pe_ready")
        b_started = sem("b_started")
        a_done = sem("a_done")
        b_done = sem("b_done")
        joined = sem("joined")
        x1_summed = sem("x1_summed")
        act_turns, sp_turns = sem("act_turns"), sem("sp_turns")

        def at(c, per_chunk, count):
            return c * per_chunk + (per_chunk + count)

        def slot(s, k, j, per_chunk):
            return ((s * CPW + k) * per_chunk + j) % 2

        with nc.Block() as block:
            @block.sync
            def _(sp):
                def load_window(at_slot, w, g, top=False, bottom=False):
                    lo, n = (R, WR + R) if top else (0, WR + R if bottom else UR)
                    first = w * (WR * W) + (0 if top else -R * W)
                    sp.dma_start(u[at_slot][:, lo:lo + n, R:R + W],
                                 x_pl[g * P:(g + 1) * P, bass.ds(first, n * W)]
                                 .rearrange("p (r w) -> p r w", w=W)).then_inc(win_loaded[at_slot], 16)

                def window(n, w, slot, g, ahead_w, ahead_g, top=False, bottom=False):
                    for k in range(CPW):
                        c = n * CPW + k
                        rows = bass.ds(w * (WR * W) + k * (CR * W), CR * W)
                        sp.wait_ge(x1_summed, c * 2 + 2)
                        passed(sp, sp_turns)
                        sp.dma_start(xc[:].rearrange("p r w -> p (r w)"), x_pl[g * P:(g + 1) * P, rows]) \
                            .then_inc(xc_loaded, 16)
                        if k == CPW - 1 and ahead_w is not None:
                            sp.wait_ge(joined, c + 2)
                            passed(sp, sp_turns)
                            load_window(slot, ahead_w, ahead_g, top, bottom)
                        sp.wait_ge(x_added, c * 16 + 32)
                        passed(sp, sp_turns)
                        sp.dma_start(x1_pl[g * P:(g + 1) * P, rows],
                                     x1[:].rearrange("p r w -> p (r w)")).then_inc(x1_stored, 16)

                sp.sem_inc(x1_stored, 16)
                sp.sem_inc(xc_loaded, 16)
                load_window(0, 0, 0, top=True)
                load_window(1, 1, 0)
                for g in range(GROUPS):
                    base = g * WIN
                    with nc.Fori(0, (WIN - 4) // 2, engines=SP_ONLY) as i:
                        for s in range(2):
                            w = i * 2 + s
                            window(w + base, w, s, g, w + 2, g)
                    ahead = min(g + 1, GROUPS - 1)
                    window(base + WIN - 4, WIN - 4, 0, g, WIN - 2, g)
                    window(base + WIN - 3, WIN - 3, 1, g, WIN - 1, g, bottom=True)
                    window(base + WIN - 2, WIN - 2, 0, g, 0, ahead, top=True)
                    window(base + WIN - 1, WIN - 1, 1, g, 1 if g + 1 < GROUPS else None, ahead)
                for s in range(2):
                    sp.wait_ge(win_loaded[s], (NWIN // 2 + 1 - s) * 16)
                sp.wait_ge(x1_stored, (NCHUNK + 1) * 16)

            @block.gpsimd
            def _(pool):
                def difference(n, buf, piece):
                    if piece == 0:
                        pool.wait_ge(u_ready, n * NU + NU)
                    lo, hi = DX_PIECES[piece]
                    nc.gpsimd.tensor_tensor(dx[buf][:, lo:hi, 0:UC - 1], u[buf][:, lo:hi, 1:UC],
                                            u[buf][:, lo:hi, 0:UC - 1], ALU.subtract).then_inc(dx_ready, 1)

                def add_x(c):
                    pool.wait_ge(joined, c + 1)
                    pool.wait_ge(xc_loaded, c * 16 + 16)
                    passed(pool, pool_turns)
                    nc.gpsimd.dma_start(x1[:].rearrange("p r w -> p (r w)"), xc[:].rearrange("p r w -> p (r w)"),
                                        accum_op=ALU.add).then_inc(x_added, 16)

                def add_dx(c, i, s, k):
                    di, base, outer, far = triples[i]
                    pool.wait_ge(t_ready, c * NTRIPLE + (i + 1))
                    passed(pool, pool_turns)
                    first = (k * CR + di) * UC + base
                    flat = dx[s][:].rearrange("p r w -> p (r w)")
                    nc.gpsimd.dma_start(t[i % 2][:, 0:RUN], flat[:, first:first + RUN], accum_op=ALU.add,
                                        max_dma_last_dim=RUN // 2 * 4).then_inc(t_added[i % 2], 16)

                pool.sem_inc(m_pool_ready, NPOOL)
                pool.wait_ge(pads_set, 1)
                for piece in range(ND):
                    difference(0, 0, piece)
                with nc.Fori(0, NWIN // 2, engines=POOL_ONLY) as i:
                    for s in range(2):
                        for k in range(CPW):
                            c = i * CH_IT + (s * CPW + k)
                            for kind, j in pool_order:
                                if kind == "dma":
                                    add_dx(c, j, s, k)
                                    continue
                                di, base, outer, far = pool_units[j]
                                pool.wait_ge(r_pool_ready, at(c, NPOOL, j + 1))
                                used = a_before[j - 2] if j >= 2 else a_before[NPOOL + j - 2] - NA
                                pool.wait_ge(a_done, at(c, NA, used))
                                nc.gpsimd.tensor_tensor(
                                    m_pool[slot(s, k, j, NPOOL)][:], r_pool[slot(s, k, j, NPOOL)][:],
                                    u[s][:, k * CR + di:k * CR + di + CR, base:base + W],
                                    ALU.add).then_inc(m_pool_ready, 1)
                                if j == 1:
                                    add_x(c)
                                if (k, j) in DX_AT:
                                    difference(i * 2 + (s + 1), 1 - s, DX_AT.index((k, j)))
                add_x(NCHUNK)
                pool.wait_ge(x_added, (NCHUNK + 1) * 16)
                for s in range(2):
                    pool.wait_ge(t_added[s], NCHUNK * NTRIPLE // 2 * 16)

            @block.tensor
            def _(pe):
                pe.sem_inc(m_pe_ready, NB)
                with nc.Fori(0, NWIN // 2, engines=PE_ONLY) as i:
                    for s in range(2):
                        for k in range(CPW):
                            c = i * CH_IT + (s * CPW + k)
                            for j, (di, base, outer, far) in enumerate(pe_units):
                                pe.wait_ge(r_pe_ready, at(c, NPE, j + 1))
                                for half in range(2):
                                    pe.wait_ge(b_done, at(c, NB, 2 * j + half - 1))
                                    for q in range(2):
                                        row = (half * 2 + q) * 2
                                        dst = m_pe[half][:, 2 * q:2 * q + 2, :]
                                        top = k * CR + di + row
                                        nc.tensor.matmul(dst, ident, u[s][:, top:top + 2, base:base + W],
                                                         start=True, stop=False)
                                        last = nc.tensor.matmul(dst, ident, r_pe[slot(s, k, j, NPE)][:, row:row + 2, :],
                                                                start=False, stop=True)
                                    last.then_inc(m_pe_ready, 1)

            @block.scalar
            def _(act):
                def normalise(n, buf, loads, piece):
                    if piece == 0:
                        act.wait_ge(win_loaded[buf], loads * 16)
                        passed(act, act_turns)
                    kind, lo, hi = NORM_PIECES[piece]
                    rows = u[buf][:, lo:hi, R:R + W]
                    nc.scalar.activation(rows, rows, ACT.Identity,
                                         bias=norm1[:, 1, kind, bass.ds(n, 1)],
                                         scale=norm1[:, 0, kind, bass.ds(n, 1)]).then_inc(u_ready, 1)

                def start_b(s, k):
                    di, dj = init_b
                    nc.scalar.activation(acc_b[:], u[s][:, k * CR + di:k * CR + di + CR, dj:dj + W], ACT.Identity,
                                         bias=nkt[:, col(di, dj):col(di, dj) + 1]).then_inc(b_started, 1)

                def sums_before(c, shift_column):
                    act.wait_ge(x_added, c * 16 + 16)
                    passed(act, act_turns)
                    shift = shift1[:, bass.ds(shift_column, 1)]
                    nc.scalar.activation(xc[:], x1[:], ACT.Identity, bias=shift,
                                         accum_out=sums1[:, 0, bass.ds(c, 1)]).then_inc(x1_summed, 1)
                    act.wait_ge(x1_summed, c * 2 + 1)
                    passed(act, act_turns)
                    nc.scalar.activation(xc[:], x1[:], ACT.Square, bias=shift,
                                         accum_out=sums1[:, 1, bass.ds(c, 1)]).then_inc(x1_summed, 1)

                act.sem_inc(r_pool_ready, NPOOL)
                act.sem_inc(r_pe_ready, NPE)
                act.wait_ge(pads_set, 1)
                for piece in range(NU):
                    normalise(0, 0, 1, piece)
                with nc.Fori(0, NWIN // 2, engines=ACT_ONLY) as i:
                    for s in range(2):
                        n = i * 2 + s
                        for k in range(CPW):
                            c = i * CH_IT + (s * CPW + k)
                            if k == 0:
                                act.wait_ge(u_ready, n * NU + NU)
                                act.wait_ge(dx_ready, n * ND + ND)
                            turn = 0
                            for kind, j in act_order:
                                if kind == "pre":
                                    di, base, outer, far = triples[j]
                                    if j >= 2:
                                        helper, done = triple_relu[j - 2]
                                        if helper == "pool":
                                            act.wait_ge(r_pool_ready, at(c, NPOOL, done + 1))
                                        else:
                                            act.wait_ge(r_pe_ready, at(c, NPE, done + 1))
                                    nc.scalar.activation(
                                        t[j % 2][:].rearrange("p (r w) -> p r w", w=UC)[:, :, 0:W],
                                        dx[s][:, k * CR + di:k * CR + di + CR, outer:outer + W], ACT.Relu,
                                        bias=gap_r[:, col(di, outer):col(di, outer) + 1]).then_inc(t_ready, 1)
                                    continue
                                if turn == START_TURN:
                                    act.wait_ge(joined, at(c, 1, 0))
                                    start_b(s, k)
                                if turn == SUMS_TURN:
                                    sums_before(c, n + k)
                                if kind == "pool":
                                    di, base, outer, far = pool_units[j]
                                    dst, ready = r_pool[slot(s, k, j, NPOOL)], r_pool_ready
                                    act.wait_ge(m_pool_ready, at(c, NPOOL, j - 1))
                                else:
                                    di, base, outer, far = pe_units[j]
                                    dst, ready = r_pe[slot(s, k, j, NPE)], r_pe_ready
                                    act.wait_ge(m_pe_ready, at(c, NB, 2 * (j - 1)))
                                right = outer > base
                                lo = base if right else outer
                                gap = gap_r if right else gap_l
                                src = dx[s][:, k * CR + di:k * CR + di + CR, lo:lo + W]
                                if far is not None:
                                    no = triple_no[(di, base, outer, far)]
                                    act.wait_ge(t_added[no % 2], c * (NTRIPLE // 2 * 16) + (no // 2 + 1) * 16)
                                    src = t[no % 2][:].rearrange("p (r w) -> p r w", w=UC)[:, :, 0:W]
                                nc.scalar.activation(
                                    dst[:], src, ACT.Relu, bias=gap[:, col(di, base):col(di, base) + 1],
                                    scale=1.0 if right else -1.0).then_inc(ready, 1)
                                if k == 0 and turn in NORM_TURNS:
                                    normalise(n + 1, 1 - s, i + (1 + s), NORM_TURNS.index(turn))
                                turn += 1
                sums_before(NCHUNK, NWIN)

            @block.vector
            def _(dve):
                nc.vector.memset(u[0][:, 0:R, R:R + W], 0.0)
                for s in range(2):
                    nc.vector.memset(u[s][:, :, 0:R], NEG)
                    nc.vector.memset(u[s][:, :, R + W:UC], NEG)
                    nc.vector.memset(dx[s][:, :, UC - 1:UC], 0.0)
                    nc.vector.memset(t[s][:].rearrange("p (r w) -> p r w", w=UC)[:, :, W:UC], 0.0)
                nc.vector.memset(xc[:], 0.0)
                nc.vector.memset(x1[:], 0.0).then_inc(pads_set, 1)
                dve.sem_inc(a_done, NA)
                dve.sem_inc(b_done, NB)
                dve.sem_inc(joined, 1)
                with nc.Fori(0, NWIN // 2, engines=DVE_ONLY) as i:
                    for s in range(2):
                        n = i * 2 + s
                        for k in range(CPW):
                            c = i * CH_IT + (s * CPW + k)
                            a_count = 0
                            for kind, j in dve_order:
                                if kind == "pe":
                                    if j == 0:
                                        dve.wait_ge(b_started, c + 1)
                                    dve.wait_ge(m_pe_ready, at(c, NB, j + 1))
                                    dve.wait_ge(b_done, at(c, NB, j - 1))
                                    di, base, outer, far = pe_units[j // 2]
                                    part = acc_b[:, (j % 2) * (CR // 2):(j % 2 + 1) * (CR // 2), :]
                                    nc.vector.scalar_tensor_tensor(
                                        out=part, in0=m_pe[j % 2][:], scalar=kt[:, col(di, base):col(di, base) + 1],
                                        in1=part, op0=ALU.subtract, op1=ALU.max).then_inc(b_done, 1)
                                    continue
                                if kind == "pool":
                                    dve.wait_ge(m_pool_ready, at(c, NPOOL, j + 1))
                                    di, base, outer, far = pool_units[j]
                                    src = m_pool[slot(s, k, j, NPOOL)][:]
                                else:
                                    di, base = rest[j]
                                    src = u[s][:, k * CR + di:k * CR + di + CR, base:base + W]
                                if a_count == 0:
                                    dve.wait_ge(joined, at(c, 1, 0))
                                    nc.vector.tensor_scalar(acc_a[:], src, kt[:, col(di, base):col(di, base) + 1],
                                                            None, ALU.subtract).then_inc(a_done, 1)
                                    a_count += 1
                                    continue
                                dve.wait_ge(a_done, at(c, NA, a_count))
                                nc.vector.scalar_tensor_tensor(
                                    out=acc_a[:], in0=src, scalar=kt[:, col(di, base):col(di, base) + 1],
                                    in1=acc_a[:], op0=ALU.subtract, op1=ALU.max).then_inc(a_done, 1)
                                a_count += 1
                            dve.wait_ge(a_done, at(c, NA, NA))
                            dve.wait_ge(b_done, at(c, NB, NB))
                            dve.wait_ge(x1_summed, c * 2 + 2)
                            dve.wait_ge(x1_stored, c * 16 + 16)
                            nc.vector.tensor_tensor(x1[:], acc_a[:], acc_b[:], ALU.max).then_inc(joined, 1)


def convolution(nc, x1_pl, h_pl, proj_w, mats, par, shift1, sums1, eps, conv_in, h_shift, h_sums):
    HR = WR + 2
    QR = 4
    PARTS = WR // QR
    rows_of = [(0, 1)] + [(1 + q * QR, 1 + (q + 1) * QR) for q in range(PARTS)] + [(HR - 1, HR)]
    NPROJ = len(rows_of)
    ident, pair_mean, channel_mean = (mats[:, m, :] for m in range(3))
    with ExitStack() as ctx:
        def sb(name, shape):
            return ctx.enter_context(nc.sbuf_tensor(name, shape, F32))

        def sem(name):
            return ctx.enter_context(nc.semaphore(name))

        xs = [sb(f"xs{s}", [P, HR, W]) for s in range(2)]
        o = [sb(f"o{s}", [P, HR, W + 2]) for s in range(2)]
        h = [sb(f"h{s}", [P, WR, W]) for s in range(2)]
        waste = sb("waste", [P, WR, W])
        tap_a = [sb(f"tap_a{s}", [P, WR, W]) for s in range(2)]
        tap_b = sb("tap_b", [P, WR, W])
        zero = sb("zero", [P, 1])
        ybar = sb("ybar", [P, 2, GROUPS])
        obar = sb("obar", [P, GROUPS])
        wsum = sb("wsum", [P, 1])
        wbd = sb("wbd", [P, P])
        wt = sb("wt", [P, P])
        wg = sb("wg", [P, GROUPS, P])
        diag = sb("diag", [P, TAPS_PE, P])
        evac = sb("evac", [P, 2, 3, NWIN])
        mom = sb("mom", [P, 2, GROUPS])
        gm = sb("gm2", [P, 2, GROUPS])
        var = sb("var2", [P, GROUPS])
        std = sb("std2", [P, GROUPS])
        cb = sb("cb", [P, GROUPS])
        pp = [ctx.enter_context(nc.psum_tensor(f"pp{s}", [P, QR, W], F32)) for s in range(2)]
        hp = [ctx.enter_context(nc.psum_tensor(f"hp{s}", [P, QR, W], F32)) for s in range(2)]

        blocks_zero = sem("blocks_zero")
        proj_loaded = sem("proj_loaded")
        step = sem("step2")
        sums_ready = sem("sums_ready")
        means_ready = sem("means_ready2")
        var_ready = sem("var_ready2")
        std_ready = sem("std_ready2")
        bias_ready = sem("bias_ready")
        wt_ready = sem("wt_ready")
        pt_ready = sem("pt_ready")
        tables_ready = sem("tables_ready")
        xs_loaded = [sem(f"xs_loaded{s}") for s in range(2)]
        projected = sem("projected")
        evacuated = sem("evacuated")
        taps_ready = sem("taps_ready")
        h_chain = sem("h_chain")
        act_taps = sem("act_taps")
        pool_adds = sem("pool_adds")
        h_stored = [sem(f"h_stored{s}") for s in range(2)]
        act_turns, sp_turns = sem("act_turns2"), sem("sp_turns2")
        h_summed = sem("h_summed")
        obar_ready = sem("obar_ready")
        hbar_ready = sem("hbar_ready")
        CHAIN = 9 - TAPS_PE - TAPS_ACT
        DVE_STEPS = PARTS * CHAIN
        HALVES = 2
        HALF_ROWS = WR // HALVES
        ADDS = 2 * HALVES

        with nc.Block() as block:
            @block.sync
            def _(sp):
                def load(w, g, slot, top=False, bottom=False):
                    lo, n = (1, HR - 1) if top else (0, HR - 1 if bottom else HR)
                    first = w * (WR * W) + (0 if top else -W)
                    sp.dma_start(xs[slot][:, lo:lo + n, :],
                                 x1_pl[g * P:(g + 1) * P, bass.ds(first, n * W)]
                                 .rearrange("p (r w) -> p r w", w=W)).then_inc(xs_loaded[slot], 16)

                def window(n, w, slot, g, ahead_w, ahead_g, top=False, bottom=False):
                    sp.wait_ge(projected, n * NPROJ + NPROJ)
                    passed(sp, sp_turns)
                    if ahead_w is not None:
                        load(ahead_w, ahead_g, slot, top, bottom)
                    sp.wait_ge(pool_adds, n * ADDS + 3 * ADDS)
                    passed(sp, sp_turns)
                    sp.dma_start(h_pl[g * P:(g + 1) * P, bass.ds(w * (WR * W), WR * W)],
                                 h[slot][:].rearrange("p r w -> p (r w)")).then_inc(h_stored[slot], 16)

                load(0, 0, 0, top=True)
                load(1, 0, 1)
                sp.wait_ge(blocks_zero, 1)
                for b in range(IMG):
                    sp.dma_start(wbd[b * CH:(b + 1) * CH, b * CH:(b + 1) * CH], proj_w).then_inc(proj_loaded, 16)
                sp.sem_inc(h_stored[0], 16)
                sp.sem_inc(h_stored[1], 16)
                for g in range(GROUPS):
                    base = g * WIN
                    with nc.Fori(0, (WIN - 4) // 2, engines=SP_ONLY) as i:
                        for s in range(2):
                            w = i * 2 + s
                            window(w + base, w, s, g, w + 2, g)
                    ahead = g + 1 < GROUPS
                    window(base + WIN - 4, WIN - 4, 0, g, WIN - 2, g)
                    window(base + WIN - 3, WIN - 3, 1, g, WIN - 1, g, bottom=True)
                    window(base + WIN - 2, WIN - 2, 0, g, 0 if ahead else None, g + 1, top=True)
                    window(base + WIN - 1, WIN - 1, 1, g, 1 if ahead else None, g + 1)
                for s in range(2):
                    sp.wait_ge(h_stored[s], (NWIN // 2 + 1) * 16)

            @block.tensor
            def _(pe):
                pe.wait_ge(sums_ready, 1)
                nc.tensor.matmul(hp[0][:, 0, 0:4], pair_mean, mom[:].rearrange("p t g -> p (t g)"),
                                 start=True, stop=True).then_inc(means_ready, 1)
                pe.wait_ge(proj_loaded, IMG * 16)
                nc.tensor.matmul(pp[0][:, 0, 0:P], wbd[:], ident, start=True, stop=True) \
                    .then_inc(pt_ready, 1)
                pe.wait_ge(wt_ready, 1)
                pe.wait_ge(bias_ready, 1)
                nc.tensor.matmul(pp[1][:, 0, 0:2 * GROUPS], wt[:], ybar[:].rearrange("p t g -> p (t g)"),
                                 start=True, stop=True).then_inc(pt_ready, 1)
                pe.wait_ge(obar_ready, 1)
                nc.tensor.matmul(hp[1][:, 0, 0:GROUPS], channel_mean, obar[:], start=True, stop=True) \
                    .then_inc(hbar_ready, 1)
                pe.wait_ge(tables_ready, 1)

                def project(n, s, g, e):
                    lo, hi = rows_of[e]
                    pe.wait_ge(evacuated, n * NPROJ + (NPROJ + e - 1))
                    for r in range(lo, hi, 2):
                        top = min(r + 2, hi)
                        last = nc.tensor.matmul(pp[e % 2][:, r - lo:top - lo, :], wg[:, g, :], xs[s][:, r:top, :],
                                                start=True, stop=True)
                    last.then_inc(projected, 1)

                def taps(n, s, q):
                    pe.wait_ge(evacuated, n * NPROJ + (NPROJ + q + 3))
                    pe.wait_ge(h_chain, n * DVE_STEPS + (DVE_STEPS + 1 + (q - 1) * CHAIN))
                    for r in range(0, QR, 2):
                        for t in range(TAPS_PE):
                            ty, tx = divmod(t, 3)
                            top = q * QR + r + ty
                            last = nc.tensor.matmul(hp[q % 2][:, r:r + 2, :], diag[:, t, :],
                                                    o[s][:, top:top + 2, tx:tx + W],
                                                    start=(t == 0), stop=(t == TAPS_PE - 1))
                    last.then_inc(taps_ready, 1)

                for g in range(GROUPS):
                    with nc.Fori(0, WIN // 2, engines=PE_ONLY) as i:
                        for s in range(2):
                            n = i * 2 + (g * WIN + s)
                            pe.wait_ge(xs_loaded[s], i * 16 + (g * WIN // 2 + 1) * 16)
                            for e in range(4):
                                project(n, s, g, e)
                            for q in range(PARTS):
                                taps(n, s, q)
                                if 4 + q < NPROJ:
                                    project(n, s, g, 4 + q)

            @block.scalar
            def _(act):
                act.wait_ge(var_ready, 1)
                nc.scalar.activation(std[:], var[:], ACT.Sqrt, bias=eps[:, 0:1]).then_inc(std_ready, 1)
                act.sem_inc(evacuated, NPROJ)
                act.sem_inc(h_summed, 1)
                act.sem_inc(act_taps, 2 * HALVES + 1)
                act.wait_ge(tables_ready, 1)

                def sum_before(n, s, which):
                    act.wait_ge(pool_adds, n * ADDS + 2 * ADDS)
                    act.wait_ge(h_summed, n * 2 + (1 + which))
                    passed(act, act_turns)
                    nc.scalar.activation(waste[:], h[1 - s][:], (ACT.Identity, ACT.Square)[which],
                                         bias=h_shift[:, 0:1],
                                         accum_out=h_sums[:, which, bass.ds(n, 1)]).then_inc(h_summed, 1)

                def evacuate(n, s, e):
                    lo, hi = rows_of[e]
                    kind = 0 if e == 0 else 2 if e == NPROJ - 1 else 1
                    act.wait_ge(projected, n * NPROJ + (e + 1))
                    passed(act, act_turns)
                    nc.scalar.activation(o[s][:, lo:hi, 1:W + 1], pp[e % 2][:, 0:hi - lo, :], ACT.Identity,
                                         bias=evac[:, 1, kind, bass.ds(n, 1)],
                                         scale=evac[:, 0, kind, bass.ds(n, 1)]).then_inc(evacuated, 1)

                def tap(n, s, half, which):
                    act.wait_ge(evacuated, n * NPROJ + (NPROJ + (4, NPROJ)[half]))
                    if which == 0:
                        act.wait_ge(pool_adds, n * ADDS + (2 * half + 2))
                        dst = tap_a[s]
                    else:
                        act.wait_ge(pool_adds, n * ADDS + (ADDS + 2 * half + 1))
                        dst = tap_b
                    t = 9 - TAPS_ACT + which
                    ty, tx = divmod(t, 3)
                    lo = half * HALF_ROWS
                    nc.scalar.activation(dst[:, lo:lo + HALF_ROWS, :],
                                         o[s][:, lo + ty:lo + ty + HALF_ROWS, tx:tx + W], ACT.Identity,
                                         bias=zero[:, 0:1],
                                         scale=par[:, COL_DW + t:COL_DW + t + 1]).then_inc(act_taps, 1)

                with nc.Fori(0, NWIN // 2, engines=ACT_ONLY) as i:
                    for s in range(2):
                        n = i * 2 + s
                        act.wait_ge(h_chain, n * DVE_STEPS + 1)
                        act.wait_ge(act_taps, n * (2 * HALVES) + 1)
                        for e in range(4):
                            evacuate(n, s, e)
                        tap(n, s, 0, 0)
                        evacuate(n, s, 4)
                        tap(n, s, 0, 1)
                        evacuate(n, s, 5)
                        sum_before(n, s, 0)
                        tap(n, s, 1, 0)
                        tap(n, s, 1, 1)
                        sum_before(n, s, 1)
                for which in range(2):
                    sum_before(NWIN, 0, which)

            @block.gpsimd
            def _(pool):
                pool.sem_inc(pool_adds, 2 * ADDS)
                pool.wait_ge(tables_ready, 1)
                with nc.Fori(0, NWIN // 2, engines=POOL_ONLY) as i:
                    for s in range(2):
                        n = i * 2 + s
                        for half in range(HALVES):
                            rows = slice(half * HALF_ROWS, (half + 1) * HALF_ROWS)
                            pool.wait_ge(act_taps, n * (2 * HALVES) + (2 * HALVES + 1 + 2 * half + 2))
                            nc.gpsimd.tensor_tensor(tap_a[s][:, rows, :], tap_a[s][:, rows, :], tap_b[:, rows, :],
                                                    ALU.add).then_inc(pool_adds, 1)
                            pool.wait_ge(pool_adds, n * ADDS + (2 * ADDS + 2 * half + 1))
                            pool.wait_ge(h_chain, n * DVE_STEPS +
                                         (DVE_STEPS + 1 + (half + 1) * (DVE_STEPS // HALVES)))
                            nc.gpsimd.tensor_tensor(h[s][:, rows, :], h[s][:, rows, :], tap_a[s][:, rows, :],
                                                    ALU.add).then_inc(pool_adds, 1)

            @block.vector
            def _(dve):
                steps = [0]

                def link(ins):
                    steps[0] += 1
                    ins.then_inc(step, 1)
                    dve.wait_ge(step, steps[0])

                nc.vector.memset(wbd[:], 0.0).then_inc(blocks_zero, 1)
                view = sums1[:, :, 1:].rearrange("p t (g c) -> p t g c", g=GROUPS)
                for t in range(2):
                    link(nc.vector.tensor_reduce(mom[:, t, :], view[:, t, :, :], mybir.AxisListType.X, ALU.add))
                nc.vector.tensor_scalar(mom[:], mom[:], 1.0 / (H * W), None, ALU.mult).then_inc(sums_ready, 1)
                nc.vector.memset(zero[:], 0.0)
                nc.vector.memset(xs[0][:, 0:1, :], 0.0)
                nc.vector.memset(h[1][:], 0.0)
                for s in range(2):
                    nc.vector.memset(o[s][:, :, 0:1], 0.0)
                    nc.vector.memset(o[s][:, :, W + 1:W + 2], 0.0)
                dve.wait_ge(means_ready, 1)
                link(nc.vector.tensor_copy(gm[:].rearrange("p t g -> p (t g)"), hp[0][:, 0, 0:4]))
                link(nc.vector.tensor_tensor(var[:], gm[:, 0, :], gm[:, 0, :], ALU.mult))
                nc.vector.tensor_tensor(var[:], gm[:, 1, :], var[:], ALU.subtract).then_inc(var_ready, 1)
                dve.wait_ge(std_ready, 1)
                link(nc.vector.reciprocal(conv_in[:, :, 0], std[:]))
                link(nc.vector.tensor_tensor(ybar[:, 0, :], mom[:, 0, :], gm[:, 0, :], ALU.subtract))
                link(nc.vector.tensor_tensor(ybar[:, 0, :], ybar[:, 0, :], conv_in[:, :, 0], ALU.mult))
                link(nc.vector.tensor_tensor(gm[:, 0, :], gm[:, 0, :], shift1[:, 1:NWIN + 1:WIN], ALU.subtract))
                link(nc.vector.scalar_tensor_tensor(out=conv_in[:, :, 1], in0=gm[:, 0, :], scalar=-1.0,
                                                    in1=conv_in[:, :, 0], op0=ALU.mult, op1=ALU.mult))
                nc.vector.tensor_copy(ybar[:, 1, :], conv_in[:, :, 1]).then_inc(bias_ready, 1)
                dve.wait_ge(pt_ready, 1)
                nc.vector.tensor_copy(wt[:], pp[0][:, 0, 0:P]).then_inc(wt_ready, 1)
                for g in range(GROUPS):
                    link(nc.vector.tensor_scalar(wg[:, g, :], pp[0][:, 0, 0:P], conv_in[:, g, 0:1], None, ALU.mult))
                for t in range(TAPS_PE):
                    link(nc.vector.tensor_scalar(diag[:, t, :], ident, par[:, COL_DW + t:COL_DW + t + 1],
                                                 None, ALU.mult))
                dve.wait_ge(pt_ready, 2)
                link(nc.vector.tensor_scalar(cb[:], pp[1][:, 0, GROUPS:2 * GROUPS], par[:, COL_PB:COL_PB + 1],
                                             None, ALU.add))
                nc.vector.tensor_scalar(obar[:], pp[1][:, 0, 0:GROUPS], par[:, COL_PB:COL_PB + 1], None,
                                        ALU.add).then_inc(obar_ready, 1)
                link(nc.vector.tensor_reduce(wsum[:], par[:, COL_DW:COL_DW + 9], mybir.AxisListType.X, ALU.add))
                dve.wait_ge(hbar_ready, 1)
                link(nc.vector.tensor_reduce(h_shift[:], hp[1][:, 0, 0:GROUPS], mybir.AxisListType.X, ALU.add))
                link(nc.vector.tensor_scalar(h_shift[:], h_shift[:], wsum[:, 0:1], -1.0 / GROUPS, ALU.mult, ALU.mult))
                link(nc.vector.memset(evac[:], 1.0))
                for g in range(GROUPS):
                    lo, hi = g * WIN, (g + 1) * WIN
                    link(nc.vector.tensor_scalar(evac[:, 1, :, lo:hi], evac[:, 1, :, lo:hi], cb[:, g:g + 1], None,
                                                 ALU.mult))
                    for kind, w in ((0, lo), (2, hi - 1)):
                        link(nc.vector.memset(evac[:, :, kind, w:w + 1], 0.0))
                nc.vector.memset(cb[:], 0.0).then_inc(tables_ready, 1)
                dve.sem_inc(h_chain, DVE_STEPS + 1)
                with nc.Fori(0, NWIN // 2, engines=DVE_ONLY) as i:
                    for s in range(2):
                        n = i * 2 + s
                        for q in range(PARTS):
                            dve.wait_ge(taps_ready, n * PARTS + (q + 1))
                            for step_no in range(CHAIN):
                                t = TAPS_PE + step_no
                                ty, tx = divmod(t, 3)
                                out = hp[q % 2][:]
                                if step_no > 0:
                                    dve.wait_ge(h_chain, n * DVE_STEPS + (DVE_STEPS + 1 + q * CHAIN + step_no))
                                if step_no == CHAIN - 1:
                                    out = h[s][:, q * QR:(q + 1) * QR, :]
                                    if q == 0:
                                        dve.wait_ge(h_stored[s], i * 16 + 16)
                                        dve.wait_ge(h_summed, n * 2 + 1)
                                nc.vector.scalar_tensor_tensor(
                                    out=out, in0=o[s][:, q * QR + ty:(q + 1) * QR + ty, tx:tx + W],
                                    scalar=par[:, COL_DW + t:COL_DW + t + 1],
                                    in1=hp[q % 2][:], op0=ALU.mult, op1=ALU.add).then_inc(h_chain, 1)


def resample(nc, x1_pl, h_pl, out_pl, mats, par, eps, conv_in, h_shift, h_sums):
    VR = 8
    NV = H // VR
    NALL = GROUPS * NV
    PR = 4
    channel_mean, same_image = mats[:, 2, :], mats[:, 3, :]
    with ExitStack() as ctx:
        def sb(name, shape):
            return ctx.enter_context(nc.sbuf_tensor(name, shape, F32))

        def sem(name):
            return ctx.enter_context(nc.semaphore(name))

        hw = [sb(f"hw{s}", [P, VR, W]) for s in range(2)]
        xw = [sb(f"xw{s}", [P, VR + 1, W]) for s in range(2)]
        y = [sb(f"y{s}", [P, VR + 1, W + 1]) for s in range(2)]
        ge = [sb(f"ge{s}", [P, VR, W]) for s in range(2)]
        z = [sb(f"z{s}", [P, VR, W]) for s in range(2)]
        dv = [sb(f"dv{s}", [P, VR, W + 1]) for s in range(2)]
        dd = [sb(f"dd{s}", [P, VR, W]) for s in range(2)]
        dh = [sb(f"dh{s}", [P, VR, W]) for s in range(2)]
        f = sb("f", [P, PR, W])
        res = [sb(f"res{s}", [P, VR, W]) for s in range(2)]
        off = sb("off", [P, 2, P])
        tab = sb("tab", [P, 6, NALL + 2])
        mv = sb("mv3", [P, 2])
        cm = sb("cm3", [P, 2])
        bn = sb("bn3", [P, 4])
        tx = [ctx.enter_context(nc.psum_tensor(f"tx{s}", [P, PR, W], F32)) for s in range(2)]
        ty = ctx.enter_context(nc.psum_tensor("ty", [P, PR, W], F32))
        ph = ctx.enter_context(nc.psum_tensor("ph", [P, PR, W], F32))

        step = sem("step3")
        moments_ready = sem("moments_ready3")
        means_ready = sem("means_ready3")
        var_ready = sem("var_ready3")
        std_ready = sem("std_ready3")
        tables_ready = sem("tables_ready3")
        hw_loaded = [sem(f"hw_loaded{s}") for s in range(2)]
        xw_loaded = [sem(f"xw_loaded{s}") for s in range(2)]
        y_ready = sem("y_ready")
        z_ready = sem("z_ready")
        ge_ready = sem("ge_ready")
        off_x = sem("off_x")
        off_y = sem("off_y")
        tanh_x = sem("tanh_x")
        tanh_y = sem("tanh_y")
        diffs = sem("diffs")
        part_x = sem("part_x")
        part_y = sem("part_y")
        chain = sem("chain3")
        stored = [sem(f"stored{s}") for s in range(2)]
        act_turns, sp_turns = sem("act_turns3"), sem("sp_turns3")

        with nc.Block() as block:
            @block.sync
            def _(sp):
                def load(w, g, slot, bottom=False):
                    n = VR if bottom else VR + 1
                    sp.dma_start(xw[slot][:, 0:n, :].rearrange("p r w -> p (r w)"),
                                 x1_pl[g * P:(g + 1) * P, bass.ds(w * (VR * W), n * W)]) \
                        .then_inc(xw_loaded[slot], 16)
                    sp.dma_start(hw[slot][:].rearrange("p r w -> p (r w)"),
                                 h_pl[g * P:(g + 1) * P, bass.ds(w * (VR * W), VR * W)]) \
                        .then_inc(hw_loaded[slot], 16)

                def window(n, w, slot, g, ahead_w, ahead_g, bottom=False):
                    sp.wait_ge(z_ready, n + 1)
                    sp.wait_ge(ge_ready, n + 1)
                    passed(sp, sp_turns)
                    load(ahead_w, ahead_g, slot, bottom)
                    sp.wait_ge(part_y, n * 2 + 5)
                    passed(sp, sp_turns)
                    sp.dma_start(out_pl[g * P:(g + 1) * P, bass.ds(w * (VR * W), VR * W)],
                                 res[slot][:].rearrange("p r w -> p (r w)")).then_inc(stored[slot], 16)

                sp.sem_inc(stored[0], 16)
                sp.sem_inc(stored[1], 16)
                load(0, 0, 0)
                load(1, 0, 1)
                for g in range(GROUPS):
                    base = g * NV
                    with nc.Fori(0, (NV - 4) // 2, engines=SP_ONLY) as i:
                        for s in range(2):
                            w = i * 2 + s
                            window(w + base, w, s, g, w + 2, g)
                    ahead = min(g + 1, GROUPS - 1)
                    window(base + NV - 4, NV - 4, 0, g, NV - 2, g)
                    window(base + NV - 3, NV - 3, 1, g, NV - 1, g, bottom=True)
                    window(base + NV - 2, NV - 2, 0, g, 0, ahead)
                    window(base + NV - 1, NV - 1, 1, g, 1, ahead)
                for s in range(2):
                    sp.wait_ge(xw_loaded[s], (NALL // 2 + 1) * 16)
                    sp.wait_ge(hw_loaded[s], (NALL // 2 + 1) * 16)
                    sp.wait_ge(stored[s], (NALL // 2 + 1) * 16)

            @block.tensor
            def _(pe):
                pe.wait_ge(moments_ready, 1)
                nc.tensor.matmul(ph[:, 0, 0:2], channel_mean, mv[:], start=True, stop=True).then_inc(means_ready, 1)
                pe.wait_ge(tables_ready, 1)
                with nc.Fori(0, NALL // 2, engines=PE_ONLY) as i:
                    for s in range(2):
                        n = i * 2 + s
                        pe.wait_ge(ge_ready, n + 1)
                        for p in range(2):
                            pe.wait_ge(part_x, n * 2 + (p + 1))
                            for r in range(0, PR, 2):
                                last = nc.tensor.matmul(tx[p][:, r:r + 2, :], off[:, 1, :],
                                                        ge[s][:, p * PR + r:p * PR + r + 2, :],
                                                        start=True, stop=True)
                            last.then_inc(off_x, 1)
                            pe.wait_ge(part_y, n * 2 + (p + 3))
                            for r in range(0, PR, 2):
                                last = nc.tensor.matmul(ty[:, r:r + 2, :], off[:, 0, :],
                                                        ge[s][:, p * PR + r:p * PR + r + 2, :],
                                                        start=True, stop=True)
                            last.then_inc(off_y, 1)

            @block.scalar
            def _(act):
                def make_y(n, s, loads):
                    act.wait_ge(xw_loaded[s], loads * 16)
                    act.wait_ge(diffs, n * 3 + 3)
                    passed(act, act_turns)
                    for k, (lo, hi) in enumerate(((0, VR), (VR, VR + 1))):
                        nc.scalar.activation(y[s][:, lo:hi, 0:W], xw[s][:, lo:hi, :], ACT.Identity,
                                             bias=tab[:, 2 * k + 1, bass.ds(n, 1)],
                                             scale=tab[:, 2 * k, bass.ds(n, 1)]).then_inc(y_ready, 1)

                def make_ge(n, s, loads):
                    act.wait_ge(hw_loaded[s], loads * 16)
                    act.wait_ge(off_y, n * 2 + 2)
                    nc.scalar.activation(ge[s][:], hw[s][:], ACT.Gelu, bias=bn[:, 3:4], scale=bn[:, 2:3]) \
                        .then_inc(ge_ready, 1)

                def make_z(n, s):
                    act.wait_ge(part_y, n * 2 + 1)
                    passed(act, act_turns)
                    nc.scalar.activation(z[s][:], xw[s][:, 0:VR, :], ACT.Identity,
                                         bias=tab[:, 5, bass.ds(n, 1)],
                                         scale=tab[:, 4, bass.ds(n, 1)]).then_inc(z_ready, 1)

                def make_tanh_x(n, p):
                    act.wait_ge(off_x, n * 2 + (p + 1))
                    nc.scalar.activation(tx[p][:], tx[p][:], ACT.Tanh).then_inc(tanh_x, 1)

                def make_tanh_y(n, p):
                    act.wait_ge(off_y, n * 2 + (p + 1 + 4))
                    nc.scalar.activation(ty[:], ty[:], ACT.Tanh).then_inc(tanh_y, 1)

                act.wait_ge(var_ready, 1)
                nc.scalar.activation(bn[:, 1:2], bn[:, 0:1], ACT.Sqrt, bias=eps[:, 0:1]).then_inc(std_ready, 1)
                act.wait_ge(tables_ready, 1)
                make_y(0, 0, 1)
                make_y(1, 1, 1)
                make_ge(0, 0, 1)
                make_z(0, 0)
                with nc.Fori(0, NALL // 2, engines=ACT_ONLY) as i:
                    for s in range(2):
                        n = i * 2 + s
                        make_tanh_x(n, 0)
                        make_tanh_y(n, 0)
                        make_tanh_x(n, 1)
                        make_z(n + 1, 1 - s)
                        make_ge(n + 1, 1 - s, i + (1 + s))
                        make_tanh_y(n, 1)
                        make_y(n + 2, s, i + 2)

            @block.gpsimd
            def _(pool):
                pool.sem_inc(diffs, 6)
                with nc.Fori(0, NALL // 2, engines=POOL_ONLY) as i:
                    for s in range(2):
                        n = i * 2 + s
                        pool.wait_ge(y_ready, n * 2 + 2)
                        pool.wait_ge(part_y, n * 2 + 1)
                        nc.gpsimd.tensor_tensor(dh[s][:], y[s][:, 0:VR, 1:W + 1], y[s][:, 0:VR, 0:W],
                                                ALU.subtract).then_inc(diffs, 1)
                        nc.gpsimd.tensor_tensor(dv[s][:], y[s][:, 1:VR + 1, :], y[s][:, 0:VR, :],
                                                ALU.subtract).then_inc(diffs, 1)
                        pool.wait_ge(diffs, n * 3 + 8)
                        nc.gpsimd.tensor_tensor(dd[s][:], dv[s][:, :, 1:W + 1], dv[s][:, :, 0:W],
                                                ALU.subtract).then_inc(diffs, 1)

            @block.vector
            def _(dve):
                steps = [0]

                def link(ins):
                    steps[0] += 1
                    ins.then_inc(step, 1)
                    dve.wait_ge(step, steps[0])

                for s in range(2):
                    nc.vector.memset(y[s][:, :, W:W + 1], 0.0)
                link(nc.vector.memset(tab[:], 1.0))
                for t in range(2):
                    link(nc.vector.tensor_reduce(mv[:, t:t + 1], h_sums[:, t, 1:], mybir.AxisListType.X, ALU.add))
                nc.vector.tensor_scalar(mv[:], mv[:], 1.0 / (GROUPS * H * W), None, ALU.mult) \
                    .then_inc(moments_ready, 1)
                dve.wait_ge(means_ready, 1)
                link(nc.vector.tensor_copy(cm[:], ph[:, 0, 0:2]))
                link(nc.vector.tensor_tensor(bn[:, 0:1], cm[:, 0:1], cm[:, 0:1], ALU.mult))
                nc.vector.tensor_tensor(bn[:, 0:1], cm[:, 1:2], bn[:, 0:1], ALU.subtract).then_inc(var_ready, 1)
                dve.wait_ge(std_ready, 1)
                link(nc.vector.reciprocal(bn[:, 2:3], bn[:, 1:2]))
                link(nc.vector.tensor_tensor(bn[:, 2:3], bn[:, 2:3], par[:, COL_BG:COL_BG + 1], ALU.mult))
                link(nc.vector.tensor_tensor(cm[:, 0:1], cm[:, 0:1], h_shift[:], ALU.subtract))
                link(nc.vector.tensor_tensor(cm[:, 0:1], cm[:, 0:1], par[:, COL_DB:COL_DB + 1], ALU.add))
                link(nc.vector.tensor_tensor(cm[:, 0:1], par[:, COL_DB:COL_DB + 1], cm[:, 0:1], ALU.subtract))
                link(nc.vector.scalar_tensor_tensor(out=bn[:, 3:4], in0=cm[:, 0:1], scalar=bn[:, 2:3],
                                                    in1=par[:, COL_BB:COL_BB + 1], op0=ALU.mult, op1=ALU.add))
                for t in range(2):
                    link(nc.vector.tensor_scalar(off[:, t, :], same_image,
                                                 par[:, COL_OFF + t:COL_OFF + t + 1], None, ALU.mult))
                for g in range(GROUPS):
                    lo, hi = g * NV, (g + 1) * NV + 2 * (g == GROUPS - 1)
                    for t in range(2):
                        for row in (t, 2 + t):
                            link(nc.vector.tensor_scalar(tab[:, row, lo:hi], tab[:, row, lo:hi],
                                                         conv_in[:, g, t:t + 1], 0.5, ALU.mult, ALU.mult))
                    link(nc.vector.tensor_scalar(tab[:, 4, lo:hi], tab[:, 4, lo:hi],
                                                 conv_in[:, g, 0:1], None, ALU.add))
                    link(nc.vector.tensor_scalar(tab[:, 5, lo:hi], tab[:, 5, lo:hi],
                                                 conv_in[:, g, 1:2], None, ALU.mult))
                    link(nc.vector.memset(tab[:, 2:4, lo + NV - 1:lo + NV], 0.0))
                dve.sem_inc(part_x, 2)
                dve.sem_inc(part_y, 3)
                dve.sem_inc(off_y, 4)
                nc.vector.memset(cm[:], 0.0).then_inc(tables_ready, 1)
                with nc.Fori(0, NALL // 2, engines=DVE_ONLY) as i:
                    for s in range(2):
                        n = i * 2 + s
                        for p in range(2):
                            at = n * 8 + 4 * p
                            rows = slice(p * PR, (p + 1) * PR)
                            part = n * 2 + (p + 1)
                            if p == 0:
                                dve.wait_ge(stored[s], i * 16 + 16)
                                dve.wait_ge(z_ready, n + 1)
                                dve.wait_ge(diffs, n * 3 + 9)
                            dve.wait_ge(tanh_x, part)
                            nc.vector.scalar_tensor_tensor(out=ph[:], in0=tx[p][:], scalar=1.0, in1=dh[s][:, rows, :],
                                                           op0=ALU.add, op1=ALU.mult).then_inc(chain, 1)
                            nc.vector.scalar_tensor_tensor(out=tx[p][:], in0=tx[p][:], scalar=1.0,
                                                           in1=dd[s][:, rows, :],
                                                           op0=ALU.add, op1=ALU.mult).then_inc(chain, 1)
                            dve.wait_ge(chain, at + 1)
                            nc.vector.tensor_tensor(res[s][:, rows, :], ph[:], z[s][:, rows, :], ALU.add) \
                                .then_inc(chain, 1)
                            dve.wait_ge(chain, at + 2)
                            nc.vector.scalar_tensor_tensor(out=f[:], in0=tx[p][:], scalar=0.5,
                                                           in1=dv[s][:, rows, 0:W],
                                                           op0=ALU.mult, op1=ALU.add).then_inc(part_x, 1)
                            dve.wait_ge(part_x, part + 2)
                            dve.wait_ge(tanh_y, part)
                            nc.vector.scalar_tensor_tensor(out=ty[:], in0=ty[:], scalar=1.0, in1=f[:],
                                                           op0=ALU.add, op1=ALU.mult).then_inc(chain, 1)
                            dve.wait_ge(chain, at + 4)
                            nc.vector.tensor_tensor(res[s][:, rows, :], ty[:], res[s][:, rows, :], ALU.add) \
                                .then_inc(part_y, 1)


def kernel(**inputs):
    import concourse.bacc as bacc
    from concourse.bass_utils import run_bass_kernel_spmd

    a = {k: np.asarray(v) for k, v in inputs.items()}
    columns = [a["L0_conv_finsler_params"], a["L1_conv_proj_b"], a["L1_conv_dw_w"], a["L1_conv_dw_b"],
               a["L1_conv_bn_g"], a["L1_conv_bn_b"], a["L1_conv_off_w"].reshape(2, CH).T]
    params = np.concatenate([c.reshape(CH, -1) for c in columns], axis=1)
    basis, mats = shape_constants()
    arrays = {
        "x_dram": np.ascontiguousarray(a["x"]),
        "params_dram": np.ascontiguousarray(np.tile(params, (IMG, 1))),
        "proj_w_dram": np.ascontiguousarray(a["L1_conv_proj_w"].reshape(CH, CH)),
        "basis_dram": basis,
        "mats_dram": mats,
    }
    nc = bacc.Bacc("TRN2", target_bir_lowering=False, num_devices=1)
    args = [nc.dram_tensor(k, v.shape, F32, kind="ExternalInput").ap() for k, v in arrays.items()]
    out = nc.dram_tensor("out_dram", a["x"].shape, F32, kind="ExternalOutput").ap()
    build(nc, *args, out)
    r = run_bass_kernel_spmd(nc, [arrays], core_ids=[0])
    return r.results[0]["out_dram"]
```
